# Optimizing a Trainium2 kernel written in Bass

```python
import numpy as np
import jax
import jax.numpy as jnp

def _softmax(x, axis=-1):
    return jax.nn.softmax(x, axis=axis)

def _gelu(x):
    return jax.nn.gelu(x, approximate=True)

def _silu(x):
    return jax.nn.silu(x)

def _sigmoid(x):
    return jax.nn.sigmoid(x)

def _layernorm(x, axis=-1, eps=1e-05):
    m = jnp.mean(x, axis=axis, keepdims=True)
    v = jnp.var(x, axis=axis, keepdims=True)
    return (x - m) / jnp.sqrt(v + eps)

def _scatter_add(tgt, idx, src, axis=0):
    return tgt.at[idx].add(src)

def _segment_sum(src, seg, n):
    return jax.ops.segment_sum(src, seg, n)
kernel_name = 'mk_vit_tower_d1_tok_img512_r4_8607b3'

def setup_inputs(seed: int=0):
    np.random.seed(seed)
    _w = jnp.asarray

    def _rec_inputs():
        import jax
        import jax.numpy as jnp
        _rk = jax.random.key(seed)
        x = -0.000356955 + 1 * jax.random.normal(jax.random.fold_in(_rk, 1), (128, 3, 64, 64), jnp.float32)
        return x
    x = _rec_inputs()

    def _L0_tok_setup():
        import jax, jax.numpy as jnp
        import numpy as np
        key = jax.random.key(seed)
        k1, k2, k3 = jax.random.split(key, 3)
        B, C, H, W = (128, 3, 224, 224)
        E, p = (128, 16)
        K = C * p * p
        img = jax.random.normal(k1, (B, C, H, W), dtype=jnp.float32)
        w = jax.random.normal(k2, (E, K), dtype=jnp.float32) * (1.0 / np.sqrt(K))
        b = jax.random.normal(k3, (E,), dtype=jnp.float32)
        return {'img': img, 'w': w, 'b': b, 'patch_size': p}
    _L0_tok_all = _L0_tok_setup()
    _L0_tok_in = {k: v for k, v in _L0_tok_all.items() if k in ('w', 'b')}
    del _L0_tok_all

    def _L0_attn_setup():
        import jax, jax.numpy as jnp
        import numpy as np
        NUM_HEADS = 8
        WINDOW_SIZES = (9, 17)
        key = jax.random.key(seed)
        k1, k2, k3 = jax.random.split(key, 3)
        B, N, C = (2, 512, 128)
        x = jax.random.normal(k1, (B, N, C), dtype=jnp.float32)
        qkv_w = jax.random.normal(k2, (3 * C, C), dtype=jnp.float32) * C ** (-0.5)
        proj_w = jax.random.normal(k3, (C, C), dtype=jnp.float32) * C ** (-0.5)
        proj_b = jnp.zeros((C,), dtype=jnp.float32)
        return {'x': x, 'qkv_w': qkv_w, 'proj_w': proj_w, 'proj_b': proj_b}
    _L0_attn_all = _L0_attn_setup()
    _L0_attn_in = {k: v for k, v in _L0_attn_all.items() if k in ('qkv_w', 'proj_w', 'proj_b')}
    del _L0_attn_all

    def _L0_ffn_setup():
        import jax, jax.numpy as jnp
        import numpy as np
        S, B, I, O, H, E, K = (128, 32, 128, 128, 128, 8, 2)

        def _expert(x_seq, Wi, Wh, b, Wo, bo):
            Bsz = x_seq.shape[1]
            Hd = Wh.shape[0]

            def step(carry, xt):
                h, c = carry
                gates = xt @ Wi + h @ Wh + b
                i_, f_, g_, o_ = jnp.split(gates, 4, axis=-1)
                c = jax.nn.sigmoid(f_) * c + jax.nn.sigmoid(i_) * jnp.tanh(g_)
                h = jax.nn.sigmoid(o_) * jnp.tanh(c)
                return ((h, c), h @ Wo + bo)
            init = (jnp.zeros((Bsz, Hd), x_seq.dtype), jnp.zeros((Bsz, Hd), x_seq.dtype))
            _, ys = jax.lax.scan(step, init, x_seq)
            return ys
        key = jax.random.key(seed)
        ks = jax.random.split(key, 6)
        s = 0.02
        return {'x': jax.random.normal(ks[0], (S, B, I), dtype=jnp.float32), 'router_w': jax.random.normal(ks[1], (I, E), dtype=jnp.float32) * s, 'router_b': jnp.zeros((E,), dtype=jnp.float32), 'Wi': jax.random.normal(ks[2], (E, I, 4 * H), dtype=jnp.float32) * s, 'Wh': jax.random.normal(ks[3], (E, H, 4 * H), dtype=jnp.float32) * s, 'b': jnp.zeros((E, 4 * H), dtype=jnp.float32), 'Wo': jax.random.normal(ks[4], (E, H, O), dtype=jnp.float32) * s, 'bo': jnp.zeros((E, O), dtype=jnp.float32)}
    _L0_ffn_all = _L0_ffn_setup()
    _L0_ffn_in = {k: v for k, v in _L0_ffn_all.items() if k in ('router_w', 'router_b', 'Wi', 'Wh', 'b', 'Wo', 'bo')}
    del _L0_ffn_all
    return {'x': x, 'L0_tok_w': _L0_tok_in['w'], 'L0_tok_b': _L0_tok_in['b'], 'L0_attn_qkv_w': _L0_attn_in['qkv_w'], 'L0_attn_proj_w': _L0_attn_in['proj_w'], 'L0_attn_proj_b': _L0_attn_in['proj_b'], 'L0_ffn_router_w': _L0_ffn_in['router_w'], 'L0_ffn_router_b': _L0_ffn_in['router_b'], 'L0_ffn_Wi': _L0_ffn_in['Wi'], 'L0_ffn_Wh': _L0_ffn_in['Wh'], 'L0_ffn_b': _L0_ffn_in['b'], 'L0_ffn_Wo': _L0_ffn_in['Wo'], 'L0_ffn_bo': _L0_ffn_in['bo']}

def reference(x, L0_tok_w, L0_tok_b, L0_attn_qkv_w, L0_attn_proj_w, L0_attn_proj_b, L0_ffn_router_w, L0_ffn_router_b, L0_ffn_Wi, L0_ffn_Wh, L0_ffn_b, L0_ffn_Wo, L0_ffn_bo):
    import jax
    import jax.numpy as jnp

    def _L0_tok_ref(img, w, b, patch_size):
        import jax, jax.numpy as jnp
        import numpy as np
        B, C, H, W = img.shape
        p = patch_size
        Hp, Wp = (H // p, W // p)
        S = Hp * Wp
        patches = img.reshape(B, C, Hp, p, Wp, p)
        patches = patches.transpose(0, 2, 4, 1, 3, 5).reshape(B, S, C * p * p)
        out = jnp.einsum('bsk,ek->bse', patches, w) + b
        return out

    def _L0_attn_ref(x, qkv_w, proj_w, proj_b):
        import jax, jax.numpy as jnp
        import numpy as np
        NUM_HEADS = 8
        WINDOW_SIZES = (9, 17)
        B, N, C = x.shape
        H = NUM_HEADS
        D = C // H
        qkv = (x @ qkv_w.T).reshape(B, N, 3, H, D)
        q = qkv[:, :, 0].transpose(0, 2, 1, 3)
        k = qkv[:, :, 1].transpose(0, 2, 1, 3)
        v = qkv[:, :, 2].transpose(0, 2, 1, 3)
        scale = D ** (-0.5)
        scores = jnp.einsum('bhnd,bhmd->bhnm', q, k) * scale
        idx = jnp.arange(N)
        dist = jnp.abs(idx[:, None] - idx[None, :])
        max_neg = -jnp.finfo(scores.dtype).max
        out = jnp.zeros_like(q)
        for ws in WINDOW_SIZES:
            mask = dist <= ws // 2
            masked = jnp.where(mask[None, None], scores, max_neg)
            attn = jax.nn.softmax(masked, axis=-1)
            out = out + jnp.einsum('bhnm,bhmd->bhnd', attn, v)
        out = out / len(WINDOW_SIZES)
        out = out.transpose(0, 2, 1, 3).reshape(B, N, C)
        return out @ proj_w.T + proj_b

    def _L0_ffn_ref(x, router_w, router_b, Wi, Wh, b, Wo, bo):
        import jax, jax.numpy as jnp
        import numpy as np
        S, B, I, O, H, E, K = (128, 32, 128, 128, 128, 8, 2)

        def _expert(x_seq, Wi, Wh, b, Wo, bo):
            Bsz = x_seq.shape[1]
            Hd = Wh.shape[0]

            def step(carry, xt):
                h, c = carry
                gates = xt @ Wi + h @ Wh + b
                i_, f_, g_, o_ = jnp.split(gates, 4, axis=-1)
                c = jax.nn.sigmoid(f_) * c + jax.nn.sigmoid(i_) * jnp.tanh(g_)
                h = jax.nn.sigmoid(o_) * jnp.tanh(c)
                return ((h, c), h @ Wo + bo)
            init = (jnp.zeros((Bsz, Hd), x_seq.dtype), jnp.zeros((Bsz, Hd), x_seq.dtype))
            _, ys = jax.lax.scan(step, init, x_seq)
            return ys
        S_, B_, I_ = x.shape
        N = S_ * B_
        flat_x = x.reshape(N, I_)
        logits = flat_x @ router_w + router_b
        top_vals, top_idx = jax.lax.top_k(logits, K)
        rw = jax.nn.softmax(top_vals, axis=1)
        mask = (top_idx.T[:, None, :] == jnp.arange(E)[None, :, None]).astype(x.dtype)
        expert_x = (mask[..., None] * flat_x[None, None]).reshape(K, E, S_, B_, I_)
        run_e = jax.vmap(_expert, in_axes=(0, 0, 0, 0, 0, 0))
        run_ke = jax.vmap(run_e, in_axes=(0, None, None, None, None, None))
        out = run_ke(expert_x, Wi, Wh, b, Wo, bo)
        out = out.reshape(K, E, N, -1)
        y = jnp.einsum('ken,nk,keno->no', mask, rw, out)
        return y.reshape(S_, B_, -1)
    h = _L0_tok_ref(x, L0_tok_w, L0_tok_b, 16)
    h = h + _L0_attn_ref(_layernorm(h, axis=-1), L0_attn_qkv_w, L0_attn_proj_w, L0_attn_proj_b)
    h = h + _L0_ffn_ref(_layernorm(h, axis=-1), L0_ffn_router_w, L0_ffn_router_b, L0_ffn_Wi, L0_ffn_Wh, L0_ffn_b, L0_ffn_Wo, L0_ffn_bo)
    return h

_drawn_inputs = setup_inputs


def setup_inputs(seed=0):
    import zlib

    import numpy as np

    out = dict(_drawn_inputs(seed))
    spreads = {'L0_attn_proj_b': (0.0, 0.1),
     'L0_ffn_router_b': (0.0, 0.293),
     'L0_ffn_b': (0.0, 0.8),
     'L0_ffn_bo': (0.0, 0.1)}
    factors = {'L0_ffn_Wi': 8.0, 'L0_ffn_Wh': 8.0, 'L0_ffn_Wo': 6.974}
    for name, (base, spread) in spreads.items():
        noise = np.random.default_rng([zlib.crc32(name.encode()), seed]).standard_normal(out[name].shape)
        drawn = base * np.exp(spread * noise) if base else spread * noise
        out[name] = jnp.asarray(drawn.astype(out[name].dtype))
    for name, factor in factors.items():
        out[name] = (out[name] * factor).astype(out[name].dtype)
    return out
```

```python
from contextlib import ExitStack

import concourse.bass as bass
from concourse import mybir

ALU = mybir.AluOpType
ACT = mybir.ActivationFunctionType
AX_X = mybir.AxisListType.X
F32 = mybir.dt.float32
I32 = mybir.dt.int32

P = 128
IMAGES = 128
PATCHES = 16
TOKENS = IMAGES * PATCHES
KCH = 6
HEADS, DH = 8, 16
EXPERTS, TOPK = 8, 2
GATES = 4 * P
ROW_TILES = 4
SUPER = ROW_TILES * P
NSUPER = TOKENS // SUPER
LN_EPS = 1e-5
RSQRT_GUESS = float(0x5F3759DF)
NEWTON = 3
BIG = 3.0e38

SEQ = EXPERTS * TOPK * PATCHES
HALF = SEQ // 2
UNROLL = 4
BODIES = IMAGES // UNROLL

C_IDENT = 0
C_BAND = 128
C_OWN = 160
C_RANK = 166
C_COLS = 174


def vit_moe_lstm_kernel(nc, patches, tok_w, tok_b, qkv_w, proj_w, proj_b, router_w, router_b,
                        w_in, w_hid, gate_b, w_out, out_b, consts, out):
    with ExitStack() as ctx:
        def sb(name, shape, dt=F32):
            return ctx.enter_context(nc.sbuf_tensor(name, shape, dt))

        def sem(name):
            return ctx.enter_context(nc.semaphore(name))

        banks = [ctx.enter_context(nc.psum_tensor(f"bank{i}", [P, 512], F32)) for i in range(4)]
        quad = ctx.enter_context(nc.psum_tensor("quad", [P, 4, 512], F32))
        lowq = None

        cst = sb("cst", [P, C_COLS])
        ident = cst[:, C_IDENT:C_IDENT + P]
        tokw = sb("tokw", [P, KCH, P])
        tokb = sb("tokb", [P, 1])
        qkvw = sb("qkvw", [P, 3, P])
        projw = sb("projw", [P, P])
        projb = sb("projb", [P, P])
        rw_sb = sb("rw_sb", [P, EXPERTS])
        rb_sb = sb("rb_sb", [P, EXPERTS])
        wi = sb("wi", [P, EXPERTS, GATES])
        wh = sb("wh", [P, EXPERTS, GATES])
        wo = sb("wo", [P, EXPERTS, P])
        bo2 = sb("bo2", [2 * EXPERTS, P])

        h2 = sb("h2", [P, NSUPER * ROW_TILES, P])
        xT = sb("xT", [P, TOKENS])
        ckT = sb("ckT", [2 * SEQ // PATCHES, TOKENS])
        mix = sb("mix", [P, EXPERTS, TOKENS])
        w0 = mix[:, 0, :]
        w0b = mix[:, 1, :]

        pt = sb("pt", [P, KCH, SUPER])
        hT = sb("hT", [P, SUPER])
        h1 = sb("h1", [P, ROW_TILES, P])
        xc = sb("xc", [P, ROW_TILES, P])
        sq = sb("sq", [P, ROW_TILES, P])
        xn = sb("xn", [P, ROW_TILES, P])
        xnT = sb("xnT", [P, SUPER])
        qT = sb("qT", [P, SUPER])
        kx = sb("kx", [P, 2, SUPER])
        vt = sb("vt", [P, ROW_TILES, P])
        s_a = sb("s_a", [P, 512])
        s_b = sb("s_b", [P, 512])
        s_e = sb("s_e", [P, 512])
        s_p = sb("s_p", [P, 512])
        ax = sb("ax", [P, 32, 32])
        axT = sb("axT", [P, 32, 32])
        oT = sb("oT", [P, SUPER])
        st = sb("st", [P, 8, 32])
        sti = sb("sti", [P, ROW_TILES], I32)
        lg = sb("lg", [P, 6, ROW_TILES, EXPERTS])
        ck = sb("ck", [P, ROW_TILES, P])

        xm = sb("xm", [P, 2, SEQ])
        hs = sb("hs", [P, 2, SEQ])
        gt = sb("gt", [P, 2, 6 * P])
        prod = sb("prod", [P, 2, 2 * P])
        thc = sb("thc", [P, 2, P])
        hc = sb("hc", [P, SEQ])
        mst = sb("mst", [P, 2, 2 * SEQ])
        cst_s = sb("cst_s", [P, 2, 2 * SEQ])

        yT = pt[:, 0, :]

        scr_c = nc.dram_tensor("scr_c", [IMAGES, 16, PATCHES], F32).ap()
        scr_m = nc.dram_tensor("scr_m", [IMAGES, 16, PATCHES], F32).ap()

        names = """const_in w_small_in w_big_in w0_in bias_in w_ready patches_in embedded hT_ready h1_tr xn_ready
            xn_tr xnT_ready qkv_ready q_copied v_copied kx_ready scores_ready even_ready odd_ready exp_ready shifted axT_ready
            heads_ready oT_ready proj_ready xn2_ready xn2_tr xn2T_ready xT_kept router_ready gap_ready gexp_ready
            ck_ready ck_tr ckT_ready scr_stored dve_done pool_done mixed shift_ready
            xm_ready hc_done zeroed ones_ready tiles_open
            yT_psum yT_ready y_tr y_ready y_out""".split()
        S = {n: sem(n) for n in names}
        pair = {n: [sem(f"{n}{g}") for g in range(2)] for n in
                "gates_ready t_ready c_ready tr_ready thc_ready h_ready m_in c_in prod_ready".split()}

        block = ctx.enter_context(nc.Block())

        patches_v = patches.rearrange("(c p) n -> p c n", p=P)
        out_v = out.rearrange("(t p) c -> p t c", p=P)

        @block.sync
        def _(sp):
            sp.dma_start(cst[:, :], consts).then_inc(S["const_in"], 16)
            sp.dma_start(tokw[:, :, :], tok_w.rearrange("(c p) n -> p c n", p=P)).then_inc(S["w_small_in"], 16)
            sp.dma_start(tokb[:, :], tok_b).then_inc(S["w_small_in"], 16)
            sp.dma_start(pt[:, :, :], patches_v[:, :, 0:SUPER]).then_inc(S["patches_in"], 16)
            sp.dma_start(qkvw[:, :, :], qkv_w.rearrange("p (t n) -> p t n", t=3)).then_inc(S["w_small_in"], 16)
            sp.dma_start(projw[:, :], proj_w).then_inc(S["w_small_in"], 16)
            sp.dma_start(projb[:, :], proj_b.partition_broadcast(P)).then_inc(S["w_small_in"], 16)
            sp.dma_start(rw_sb[:, :], router_w).then_inc(S["w_small_in"], 16)
            sp.dma_start(rb_sb[:, :], router_b.partition_broadcast(P)).then_inc(S["w_small_in"], 16)
            sp.dma_start(wi[:, :, :], w_in.rearrange("e p n -> p e n")).then_inc(S["w_big_in"], 16)
            sp.dma_start(wh[:, :, :], w_hid.rearrange("e p n -> p e n")).then_inc(S["w_big_in"], 16)
            for half, dst in enumerate((w0, w0b)):
                sp.dma_start(dst.rearrange("p (e n) -> p e n", n=GATES),
                             w_in[4 * half:4 * half + 4, 0, :].partition_broadcast(P)).then_inc(S["w_big_in"], 16)
            sp.dma_start(wo[:, :, :], w_out.rearrange("e p n -> p e n")).then_inc(S["w_big_in"], 16)
            sp.dma_start(bo2[:, :], out_b).then_inc(S["w_big_in"], 16)
            sp.wait_ge(S["shift_ready"], 1)
            sp.dma_start(wi[0:1, :, :], gate_b.rearrange("e n -> (e n)").partition_broadcast(1)
                         .rearrange("o (e n) -> o e n", e=EXPERTS)).then_inc(S["bias_in"], 16)

            def store_routing(i):
                for r, scr in ((0, scr_c), (16, scr_m)):
                    sp.dma_start(scr[bass.ds(i * 32, 32), :, :].rearrange("s k b -> k s b"),
                                 ckT[r:r + 16, bass.ds(i * SUPER, SUPER)].rearrange("k (s b) -> k s b", b=PATCHES)
                                 ).then_inc(S["scr_stored"], 16)

            with sp.Fori(0, NSUPER - 1) as i:
                sp.wait_ge(S["embedded"], i + 1)
                sp.dma_start(pt[:, :, :], patches_v[:, :, bass.ds((i + 1) * SUPER, SUPER)]
                             ).then_inc(S["patches_in"], 16)
                sp.wait_ge(S["ckT_ready"], i + 1)
                store_routing(i)
            sp.wait_ge(S["ckT_ready"], NSUPER)
            store_routing(NSUPER - 1)
            sp.wait_ge(S["scr_stored"], 32 * NSUPER)

            def load_masks(j, half):
                src = scr_m[bass.ds(j * UNROLL + 2 * half, 2), :, :].rearrange("s k b -> (s k b)")
                sp.dma_start(mst[1:P, half, :], src.partition_broadcast(P - 1)).then_inc(pair["m_in"][half], 16)

            def load_weights(j, half):
                src = scr_c[bass.ds(j * UNROLL + 2 * half, 2), :, :].rearrange("s k b -> (s k b)")
                sp.dma_start(cst_s[:, half, :], src.partition_broadcast(P)).then_inc(pair["c_in"][half], 16)

            for half in range(2):
                load_masks(0, half)
                load_weights(0, half)
            with sp.Fori(0, BODIES - 1) as j:
                sp.wait_ge(S["xm_ready"], j * UNROLL + 2)
                load_masks(j + 1, 0)
                sp.wait_ge(S["xm_ready"], j * UNROLL + 4)
                load_masks(j + 1, 1)
                sp.wait_ge(S["hc_done"], j * UNROLL + 2 + 2)
                load_weights(j + 1, 0)
                sp.wait_ge(S["hc_done"], j * UNROLL + 4 + 2)
                load_weights(j + 1, 1)
            with sp.Fori(0, NSUPER) as w:
                sp.wait_ge(S["y_ready"], w + 2)
                rows = bass.ds(w * ROW_TILES, ROW_TILES)
                sp.dma_start(out_v[:, rows, :], h2[:, rows, :]).then_inc(S["y_out"], 16)
            sp.wait_ge(S["y_out"], 16 * NSUPER)

        @block.tensor
        def _(pe):
            pe.wait_ge(S["const_in"], 16)
            pe.wait_ge(S["w_small_in"], 16 * 7)
            with pe.Fori(0, NSUPER) as i:
                pe.wait_ge(S["patches_in"], (i + 1) * 16)
                for c in range(KCH):
                    m = pe.matmul(banks[0][:, :], tokw[:, c, :], pt[:, c, :], start=c == 0, stop=c == KCH - 1)
                m.then_inc(S["embedded"], 1)
                pe.wait_ge(S["hT_ready"], i + 1)
                for t in range(ROW_TILES):
                    m = pe.transpose(banks[1][:, t * P:(t + 1) * P], hT[:, t * P:(t + 1) * P], ident)
                m.then_inc(S["h1_tr"], 1)
                pe.wait_ge(S["xn_ready"], i + 1)
                for t in range(ROW_TILES):
                    m = pe.transpose(banks[2][:, t * P:(t + 1) * P], xn[:, t, :], ident)
                m.then_inc(S["xn_tr"], 1)
                pe.wait_ge(S["xnT_ready"], i + 1)
                pe.matmul(banks[0][:, :], qkvw[:, 0, :], xnT[:, :], start=True, stop=True)
                pe.matmul(banks[1][:, :], qkvw[:, 1, :], xnT[:, :], start=True, stop=True)
                for t in range(ROW_TILES):
                    m = pe.matmul(banks[2][:, t * P:(t + 1) * P], xnT[:, t * P:(t + 1) * P], qkvw[:, 2, :],
                                  start=True, stop=True)
                m.then_inc(S["qkv_ready"], 1)
                pe.wait_ge(S["q_copied"], i + 1)
                pe.wait_ge(S["kx_ready"], i + 1)
                pe.sem_inc(S["tiles_open"])
                for t in range(ROW_TILES):
                    for c in range(4):
                        for j in range(4):
                            tok = slice(t * P + 32 * j, t * P + 32 * j + 32)
                            m = pe.matmul(quad[32 * j:32 * j + 32, c, t * 64:(t + 1) * 64],
                                          qT[32 * c:32 * c + 32, tok], kx[32 * c:32 * c + 32, :, tok],
                                          start=True, stop=True)
                m.then_inc(S["scores_ready"], 1)
                pe.wait_ge(S["axT_ready"], i + 1)
                pe.wait_ge(S["v_copied"], i + 1)
                pe.sem_inc(S["tiles_open"])
                for t in range(ROW_TILES):
                    for j in range(4):
                        for c in range(4):
                            b0 = c * 8 + t * 2
                            m = pe.matmul(banks[j][32 * c:32 * c + 32, t * 64:(t + 1) * 64],
                                          vt[32 * j:32 * j + 32, t, 32 * c:32 * c + 32],
                                          axT[32 * j:32 * j + 32, b0:b0 + 2, :], start=True, stop=True)
                m.then_inc(S["heads_ready"], 1)
                pe.wait_ge(S["oT_ready"], i + 1)
                for t in range(ROW_TILES):
                    m = pe.matmul(quad[:, 0, t * P:(t + 1) * P], oT[:, t * P:(t + 1) * P], projw[:, :],
                                  start=True, stop=True)
                m.then_inc(S["proj_ready"], 1)
                pe.wait_ge(S["xn2_ready"], i + 1)
                for t in range(ROW_TILES):
                    m = pe.transpose(quad[:, 1, t * P:(t + 1) * P], xn[:, t, :], ident)
                m.then_inc(S["xn2_tr"], 1)
                pe.wait_ge(S["xn2T_ready"], i + 1)
                for t in range(ROW_TILES):
                    m = pe.matmul(quad[:, 2, t * EXPERTS:(t + 1) * EXPERTS], xnT[:, t * P:(t + 1) * P], rw_sb[:, :],
                                  start=True, stop=True)
                m.then_inc(S["router_ready"], 1)
                pe.wait_ge(S["ck_ready"], i + 1)
                for t in range(ROW_TILES):
                    m = pe.transpose(quad[:, 3, t * P:(t + 1) * P], ck[:, t, :], ident)
                m.then_inc(S["ck_tr"], 1)

            def gates(g, par):
                return banks[2 * g + par]

            def from_inputs(g, s, par):
                pe.wait_ge(S["xm_ready"], s + 1)
                for q in range(4):
                    e = 4 * g + q
                    pe.matmul(gates(g, par)[32 * q:32 * q + 32, :], xm[:, par, 32 * e:32 * e + 32], wi[:, e, :],
                              start=True, stop=False)

            def from_hidden(g, s, par):
                pe.wait_ge(pair["h_ready"][g], s + 1)
                for q in range(4):
                    e = 4 * g + q
                    m = pe.matmul(gates(g, par)[32 * q:32 * q + 32, :], hs[:, 1 - par, 32 * e:32 * e + 32],
                                  wh[:, e, :], start=False, stop=True)
                m.then_inc(pair["gates_ready"][g], 1)

            def turn(g, s):
                pe.wait_ge(pair["t_ready"][g], s + 1)
                pe.transpose(quad[:, g, 0:P], gt[:, g, 3 * P:4 * P], ident)
                pe.wait_ge(pair["c_ready"][g], s + 1)
                pe.transpose(quad[:, g, P:2 * P], gt[:, g, 4 * P:5 * P], ident).then_inc(pair["tr_ready"][g], 1)

            pe.wait_ge(S["w_ready"], 1)
            pe.wait_ge(S["ckT_ready"], NSUPER)
            from_inputs(0, 0, 0)
            from_inputs(1, 0, 0)
            from_hidden(0, 0, 0)

            def steps(base, last):
                for u in range(UNROLL):
                    s, par = base + u, u % 2
                    end = last and u == UNROLL - 1
                    if not end:
                        from_inputs(0, s + 1, 1 - par)
                    from_hidden(1, s, par)
                    turn(0, s)
                    if not end:
                        from_inputs(1, s + 1, 1 - par)
                        from_hidden(0, s + 1, 1 - par)
                    turn(1, s)

            with pe.Fori(0, BODIES - 1) as j:
                steps(j * UNROLL, False)
            steps((BODIES - 1) * UNROLL, True)

            pe.wait_ge(S["hc_done"], IMAGES + 2)
            pe.wait_ge(S["y_ready"], 1)
            with pe.Fori(0, NSUPER) as w:
                for e in range(EXPERTS):
                    pe.matmul(banks[0][:, :], wo[:, e, :], mix[:, e, bass.ds(w * SUPER, SUPER)],
                              start=e == 0, stop=False)
                pe.matmul(banks[0][:, :], bo2[:, :], ckT[0:2 * EXPERTS, bass.ds(w * SUPER, SUPER)],
                          start=False, stop=True).then_inc(S["yT_psum"], 1)
                pe.wait_ge(S["yT_ready"], w + 1)
                pe.wait_ge(S["y_ready"], w + 1)
                for t in range(ROW_TILES):
                    m = pe.transpose(banks[1][:, t * P:(t + 1) * P], pt[:, 0, t * P:(t + 1) * P], ident)
                m.then_inc(S["y_tr"], 1)

        @block.scalar
        def _(act):
            act.wait_ge(S["w_small_in"], 16 * 7)
            with act.Fori(0, NSUPER) as i:
                act.wait_ge(S["embedded"], i + 1)
                act.activation(hT[:, :], banks[0][:, :], ACT.Identity, bias=tokb[:, 0:1]).then_inc(S["hT_ready"], 1)
                act.wait_ge(S["xn_tr"], i + 1)
                act.wait_ge(S["xT_kept"], i + 1)
                act.activation(xnT[:, :], banks[2][:, :], ACT.Copy).then_inc(S["xnT_ready"], 1)
                act.wait_ge(S["qkv_ready"], i + 1)
                act.activation(qT[:, :], banks[0][:, :], ACT.Copy).then_inc(S["q_copied"], 1)
                act.activation(vt[:, :, :].rearrange("p t c -> p (t c)"), banks[2][:, :], ACT.Copy
                               ).then_inc(S["v_copied"], 1)
                act.wait_ge(S["even_ready"], i + 1)
                act.activation(s_e[:, :].rearrange("p (c r k) -> p c r k", c=4, k=PATCHES),
                               quad[:, :, 0:256].rearrange("p c (r i k) -> p c r i k", i=2, k=PATCHES)[:, :, :, 1, :],
                               ACT.Identity, scale=cst[:, C_OWN + 3:C_OWN + 4]).then_inc(S["odd_ready"], 1)
                for w in range(2):
                    act.wait_ge(S["shifted"], i * 2 + (w + 1))
                    act.activation(s_e[:, :], s_b[:, :], ACT.Exp).then_inc(S["exp_ready"], 1)
                act.wait_ge(S["xn2_tr"], i + 1)
                act.activation(xnT[:, :], quad[:, 1, :], ACT.Copy).then_inc(S["xn2T_ready"], 1)
                act.wait_ge(S["gap_ready"], i + 1)
                act.activation(st[:, 7, 0:4], st[:, 6, 0:4], ACT.Exp).then_inc(S["gexp_ready"], 1)
                act.wait_ge(S["ck_tr"], i + 1)
                act.activation(ckT[:, bass.ds(i * SUPER, SUPER)], quad[0:32, 3, :], ACT.Copy
                               ).then_inc(S["ckT_ready"], 1)

            def gate_tanh(g, s, par):
                act.wait_ge(pair["gates_ready"][g], s + 1)
                act.activation(gt[:, g, 0:GATES], banks[2 * g + par][:, :], ACT.Tanh).then_inc(pair["t_ready"][g], 1)

            def cell_tanh(g, s):
                act.wait_ge(pair["tr_ready"][g], s + 1)
                act.activation(thc[:, g, :], quad[:, g, P:2 * P], ACT.Tanh, scale=0.5
                               ).then_inc(pair["thc_ready"][g], 1)

            gate_tanh(0, 0, 0)

            def steps(base, last):
                for u in range(UNROLL):
                    s, par = base + u, u % 2
                    cell_tanh(0, s)
                    gate_tanh(1, s, par)
                    cell_tanh(1, s)
                    if not (last and u == UNROLL - 1):
                        gate_tanh(0, s + 1, 1 - par)

            with act.Fori(0, BODIES - 1) as j:
                steps(j * UNROLL, False)
            steps((BODIES - 1) * UNROLL, True)
            with act.Fori(0, NSUPER) as w:
                act.wait_ge(S["yT_psum"], w + 1)
                act.activation(yT, banks[0][:, :], ACT.Copy).then_inc(S["yT_ready"], 1)

        @block.vector
        def _(dve):
            done = S["dve_done"]

            def chain(base):
                count = [0]

                def own(ins):
                    count[0] += 1
                    ins.then_inc(done, 1)
                    dve.wait_ge(done, base + count[0])
                return own, count

            own, count = chain(0)
            own(dve.memset(ck[:, :, :], 0.0))
            dve.wait_ge(S["w_big_in"], 16 * 6)
            own(dve.tensor_tensor(wi[:, 0:4, :].rearrange("p e n -> p (e n)"),
                                  wi[:, 0:4, :].rearrange("p e n -> p (e n)"), w0, ALU.subtract))
            dve.tensor_tensor(wi[:, 4:8, :].rearrange("p e n -> p (e n)"),
                              wi[:, 4:8, :].rearrange("p e n -> p (e n)"), w0b, ALU.subtract
                              ).then_inc(S["shift_ready"], 1)
            own(dve.tensor_scalar(bo2[:, :], bo2[:, :], 2.0, None, ALU.mult))
            own(dve.tensor_scalar(wh[:, :, 0:2 * P], wh[:, :, 0:2 * P], 0.25, None, ALU.mult))
            own(dve.tensor_scalar(wh[:, :, 2 * P:3 * P], wh[:, :, 2 * P:3 * P], 0.5, None, ALU.mult))
            own(dve.tensor_scalar(wh[:, :, 3 * P:], wh[:, :, 3 * P:], 0.25, None, ALU.mult))
            dve.wait_ge(S["shift_ready"], 1)
            dve.wait_ge(S["bias_in"], 16)
            own(dve.tensor_scalar(wi[:, :, 0:2 * P], wi[:, :, 0:2 * P], 0.5, None, ALU.mult))
            own(dve.tensor_scalar(wi[:, :, 3 * P:], wi[:, :, 3 * P:], 0.5, None, ALU.mult))
            dve.memset(gt[:, :, 4 * P:], 0.0).then_inc(S["w_ready"], 1)
            dve.memset(hs[:, :, 0:HALF], 0.0).then_inc(pair["h_ready"][0], 1)
            dve.memset(hs[:, :, HALF:], 0.0).then_inc(pair["h_ready"][1], 1)
            dve.wait_ge(S["w_ready"], 1)
            setup = count[0]

            def rows(a):
                return a.unsqueeze(2).to_broadcast([P, ROW_TILES, P])

            def layernorm(own, src):
                own(dve.tensor_reduce(st[:, 0, 0:4], src, AX_X, ALU.add))
                own(dve.tensor_scalar(st[:, 1, 0:4], st[:, 0, 0:4], 1.0 / P, None, ALU.mult))
                own(dve.tensor_tensor(xc[:, :, :], src, rows(st[:, 1, 0:4]), ALU.subtract))
                own(dve.tensor_tensor(sq[:, :, :], xc[:, :, :], xc[:, :, :], ALU.mult))
                own(dve.tensor_reduce(st[:, 2, 0:4], sq[:, :, :], AX_X, ALU.add))
                own(dve.tensor_scalar(st[:, 3, 0:4], st[:, 2, 0:4], 1.0 / P, LN_EPS, ALU.mult, ALU.add))
                var, root, z, w = st[:, 3, 0:4], st[:, 4, 0:4], st[:, 5, 0:4], st[:, 5, 8:12]
                own(dve.tensor_scalar(sti[:, 0:4], st[:, 3, 0:4].bitcast(I32), 1, None, ALU.logical_shift_right))
                own(dve.tensor_scalar(root.bitcast(I32), sti[:, 0:4], -1.0, RSQRT_GUESS, ALU.mult, ALU.add))
                for _ in range(NEWTON):
                    own(dve.scalar_tensor_tensor(out=z, in0=root, scalar=-0.5, in1=root, op0=ALU.mult,
                                                 op1=ALU.mult))
                    own(dve.tensor_tensor(w, z, var, ALU.mult))
                    own(dve.scalar_tensor_tensor(out=root, in0=w, scalar=1.5, in1=root, op0=ALU.add, op1=ALU.mult))
                return dve.tensor_tensor(xn[:, :, :], xc[:, :, :], rows(st[:, 4, 0:4]), ALU.mult)

            def keys(a):
                return a.rearrange("p (r k) -> p r k", k=PATCHES)

            def own_col(n):
                return cst[:, C_OWN + n:C_OWN + n + 1]

            LINKS = 77
            dve.wait_ge(S["const_in"], 16)
            dve.wait_ge(S["w_small_in"], 16 * 7)
            with dve.Fori(0, NSUPER) as i:
                own, count = chain(i * LINKS + setup)
                dve.wait_ge(S["h1_tr"], i + 1)
                h1_p = banks[1][:, :].rearrange("p (t c) -> p t c", c=P)
                own(dve.tensor_tensor(h1[:, :, :], h1_p, projb[:, :].unsqueeze(1).to_broadcast([P, ROW_TILES, P]),
                                      ALU.add))
                layernorm(own, h1_p).then_inc(S["xn_ready"], 1)
                dve.wait_ge(S["qkv_ready"], i + 1)
                own(dve.tensor_scalar(kx[:, 0, :], banks[1][:, :], own_col(0), None, ALU.mult))
                dve.tensor_scalar(kx[:, 1, :], banks[1][:, :], own_col(1), None, ALU.mult).then_inc(S["kx_ready"], 1)
                dve.wait_ge(S["scores_ready"], i + 1)
                s_all = quad[:, :, 0:256].rearrange("p c (r i k) -> p c r i k", i=2, k=PATCHES)
                s_b4 = s_b[:, :].rearrange("p (c r k) -> p c r k", c=4, k=PATCHES)
                dve.tensor_scalar(s_b4, s_all[:, :, :, 0, :], own_col(2), None, ALU.mult).then_inc(S["even_ready"], 1)
                dve.wait_ge(S["even_ready"], i + 1)
                dve.wait_ge(S["odd_ready"], i + 1)
                own(dve.tensor_tensor(s_a[:, :], s_b[:, :], s_e[:, :], ALU.add))
                for w in range(2):
                    band = cst[:, C_BAND + w * PATCHES:C_BAND + (w + 1) * PATCHES] \
                        .unsqueeze(1).to_broadcast([P, 32, PATCHES])
                    own(dve.tensor_tensor(keys(s_b[:, :]), keys(s_a[:, :]), band, ALU.add))
                    own(dve.tensor_reduce(st[:, 0, :], keys(s_b[:, :]), AX_X, ALU.max))
                    dve.tensor_tensor(keys(s_b[:, :]), keys(s_b[:, :]),
                                      st[:, 0, :].unsqueeze(2).to_broadcast([P, 32, PATCHES]), ALU.subtract
                                      ).then_inc(S["shifted"], 1)
                    dve.wait_ge(S["exp_ready"], i * 2 + (w + 1))
                    own(dve.tensor_reduce(st[:, 1, :], keys(s_e[:, :]), AX_X, ALU.add))
                    own(dve.reciprocal(st[:, 2, :], st[:, 1, :]))
                    dst = s_p if w == 0 else s_e
                    own(dve.tensor_tensor(keys(dst[:, :]), keys(s_e[:, :]),
                                          st[:, 2, :].unsqueeze(2).to_broadcast([P, 32, PATCHES]), ALU.mult))
                own(dve.tensor_tensor(s_p[:, :], s_p[:, :], s_e[:, :], ALU.add))
                for h in range(2):
                    own(dve.tensor_scalar(ax[:, :, h * PATCHES:(h + 1) * PATCHES], keys(s_p[:, :]), own_col(2 + h),
                                          None, ALU.mult))
                dve.transpose(axT[:, :, :].rearrange("p a b -> p (a b)"), ax[:, :, :].rearrange("p a b -> p (a b)")
                              ).then_inc(S["axT_ready"], 1)
                dve.wait_ge(S["heads_ready"], i + 1)
                for j in range(4):
                    o_j = banks[j][:, 0:256].rearrange("p (t h q) -> p t h q", t=4, h=2)
                    d_j = oT[:, :].rearrange("p (t j q) -> p t j q", t=4, j=4)[:, :, j, :]
                    own(dve.tensor_scalar(d_j, o_j[:, :, 0, :], own_col(4), None, ALU.mult))
                    ins = dve.scalar_tensor_tensor(out=d_j, in0=o_j[:, :, 1, :], scalar=own_col(5), in1=d_j,
                                                   op0=ALU.mult, op1=ALU.add)
                    if j < 3:
                        own(ins)
                    else:
                        ins.then_inc(S["oT_ready"], 1)
                dve.wait_ge(S["proj_ready"], i + 1)
                proj = quad[:, 0, :].rearrange("p (t c) -> p t c", c=P)
                h2_i = h2[:, bass.ds(i * ROW_TILES, ROW_TILES), :]
                own(dve.tensor_tensor(h1[:, :, :], h1[:, :, :], proj, ALU.add))
                own(dve.tensor_copy(h2_i, h1[:, :, :]))
                layernorm(own, h1[:, :, :]).then_inc(S["xn2_ready"], 1)
                dve.wait_ge(S["router_ready"], i + 1)
                lgt, sc, oh1, oh2, l2, eq = (lg[:, n, :, :] for n in range(6))

                def cols(a):
                    return a.unsqueeze(2).to_broadcast([P, ROW_TILES, EXPERTS])

                rank = cst[:, C_RANK:C_RANK + EXPERTS].unsqueeze(1).to_broadcast([P, ROW_TILES, EXPERTS])
                own(dve.tensor_tensor(lgt, quad[:, 2, 0:32].rearrange("p (t e) -> p t e", e=EXPERTS),
                                      rb_sb[:, :].unsqueeze(1).to_broadcast([P, ROW_TILES, EXPERTS]), ALU.add))
                for n, (src, oh) in enumerate(((lgt, oh1), (l2, oh2))):
                    own(dve.tensor_reduce(st[:, n, 0:4], src, AX_X, ALU.max))
                    own(dve.tensor_tensor(eq, src, cols(st[:, n, 0:4]), ALU.is_equal))
                    own(dve.tensor_tensor(sc, eq, rank, ALU.mult))
                    own(dve.tensor_reduce(st[:, 2, 0:4], sc, AX_X, ALU.max))
                    own(dve.tensor_tensor(oh, sc, cols(st[:, 2, 0:4]), ALU.is_equal))
                    if n == 0:
                        own(dve.scalar_tensor_tensor(out=l2, in0=oh1, scalar=-BIG, in1=lgt, op0=ALU.mult,
                                                     op1=ALU.add))
                dve.tensor_tensor(st[:, 6, 0:4], st[:, 1, 0:4], st[:, 0, 0:4], ALU.subtract
                                  ).then_inc(S["gap_ready"], 1)
                dve.wait_ge(S["gexp_ready"], i + 1)
                own(dve.tensor_scalar(st[:, 3, 0:4], st[:, 7, 0:4], 1.0, None, ALU.add))
                own(dve.reciprocal(st[:, 4, 0:4], st[:, 3, 0:4]))
                own(dve.tensor_tensor(st[:, 5, 0:4], st[:, 7, 0:4], st[:, 4, 0:4], ALU.mult))
                for k, oh in enumerate((oh1, oh2)):
                    w_k = ck[:, :, 0:16].rearrange("p t (e k) -> p t e k", k=2)[:, :, :, k]
                    m_k = ck[:, :, 16:32].rearrange("p t (e k) -> p t e k", k=2)[:, :, :, k]
                    own(dve.scalar_tensor_tensor(out=w_k, in0=oh, scalar=0.5, in1=cols(st[:, 4 + k, 0:4]),
                                                 op0=ALU.mult, op1=ALU.mult))
                    copied = dve.tensor_copy(m_k, oh)
                    if k == 0:
                        own(copied)
                copied.then_inc(S["ck_ready"], 1)
            assert count[0] == LINKS, count[0]

            def cell_update(g, s):
                dve.wait_ge(pair["t_ready"][g], s + 1)
                dve.scalar_tensor_tensor(out=prod[:, g, :].rearrange("p (a u) -> p a u", u=P),
                                         in0=gt[:, g, 0:2 * P].rearrange("p (a u) -> p a u", u=P), scalar=1.0,
                                         in1=gt[:, g, 2 * P:].rearrange("p (a u) -> p a u", a=2)[:, :, 0:P],
                                         op0=ALU.add, op1=ALU.mult).then_inc(pair["prod_ready"][g], 1)
                dve.wait_ge(pair["prod_ready"][g], s + 1)
                dve.scalar_tensor_tensor(out=gt[:, g, 4 * P:5 * P], in0=prod[:, g, P:], scalar=0.5,
                                         in1=prod[:, g, 0:P], op0=ALU.mult, op1=ALU.add
                                         ).then_inc(pair["c_ready"][g], 1)

            def hidden(g, s, par):
                dve.wait_ge(pair["thc_ready"][g], s + 1)
                dve.wait_ge(S["hc_done"], s + 1)
                dve.scalar_tensor_tensor(out=hs[:, par, g * HALF:(g + 1) * HALF], in0=quad[:, g, 0:P], scalar=1.0,
                                         in1=thc[:, g, :], op0=ALU.add, op1=ALU.mult
                                         ).then_inc(pair["h_ready"][g], 1)

            cell_update(0, 0)

            def steps(base, last):
                for u in range(UNROLL):
                    s, par = base + u, u % 2
                    hidden(0, s, par)
                    cell_update(1, s)
                    hidden(1, s, par)
                    if not (last and u == UNROLL - 1):
                        cell_update(0, s + 1)

            with dve.Fori(0, BODIES - 1) as j:
                steps(j * UNROLL, False)
            steps((BODIES - 1) * UNROLL, True)

            with dve.Fori(0, NSUPER) as w:
                dve.wait_ge(S["y_tr"], w + 1)
                rows = h2[:, bass.ds(w * ROW_TILES, ROW_TILES), :]
                dve.tensor_tensor(rows, banks[1][:, :].rearrange("p (t c) -> p t c", c=P), rows, ALU.add
                                  ).then_inc(S["y_ready"], 1)

        @block.gpsimd
        def _(pool):
            pool.memset(mst[0:1, :, :], 1.0).then_inc(S["xT_kept"], 1)
            pool.memset(hc[:, 0:P], 0.0).then_inc(S["hc_done"], 2)
            pool.memset(hc[:, P:], 0.0).then_inc(S["mixed"], 1)
            with pool.Fori(0, NSUPER) as i:
                pool.wait_ge(S["xn2T_ready"], i + 1)
                pool.tensor_copy(xT[:, bass.ds(i * SUPER, SUPER)], xnT[:, :]).then_inc(S["xT_kept"], 1)
            pool.wait_ge(S["xT_kept"], NSUPER + 1)
            pool.memset(xT[0:1, :], 1.0).then_inc(S["ones_ready"], 1)
            pool.wait_ge(S["ones_ready"], 1)

            def masked_input(s, par, half, in_half, count):
                pool.wait_ge(pair["m_in"][half], count)
                x_s = xT[:, bass.ds(s * PATCHES, PATCHES)].unsqueeze(1).to_broadcast([P, 16, PATCHES])
                pool.tensor_tensor(xm[:, par, :].rearrange("p (k b) -> p k b", b=PATCHES), x_s,
                                   mst[:, half, in_half * SEQ:(in_half + 1) * SEQ]
                                   .rearrange("p (k b) -> p k b", b=PATCHES), ALU.mult).then_inc(S["xm_ready"], 1)

            def weighted_state(s, par, half, in_half, count):
                pool.wait_ge(pair["h_ready"][0], s + 2)
                pool.wait_ge(pair["h_ready"][1], s + 2)
                pool.wait_ge(pair["c_in"][half], count)
                pool.wait_ge(S["mixed"], s + 1)
                pool.tensor_tensor(hc[:, :], hs[:, par, :], cst_s[:, half, in_half * SEQ:(in_half + 1) * SEQ],
                                   ALU.mult).then_inc(S["hc_done"], 1)
                pool.wait_ge(S["hc_done"], s + 1 + 2)
                by_choice = hc[:, :].rearrange("p (e k b) -> p e k b", k=2, b=PATCHES)
                pool.tensor_tensor(mix[:, :, bass.ds(s * PATCHES, PATCHES)], by_choice[:, :, 0, :],
                                   by_choice[:, :, 1, :], ALU.add).then_inc(S["mixed"], 1)

            masked_input(0, 0, 0, 0, 16)
            masked_input(1, 1, 0, 1, 16)

            def steps(j, last):
                for u in range(UNROLL):
                    s, par = j * UNROLL + u, u % 2
                    if u < 2 or not last:
                        pool.wait_ge(pair["gates_ready"][1], s + 1)
                        masked_input(s + 2, par, (u // 2 + 1) % 2, par, j * 16 + (16 if u < 2 else 32))
                    weighted_state(s, par, u // 2, par, j * 16 + 16)

            with pool.Fori(0, BODIES - 1) as j:
                steps(j, False)
            steps(BODIES - 1, True)
            pool.wait_ge(S["mixed"], IMAGES + 1)
            pool.memset(hc[:, :], 0.0).then_inc(S["y_ready"], 1)


def kernel(x, L0_tok_w, L0_tok_b, L0_attn_qkv_w, L0_attn_proj_w, L0_attn_proj_b, L0_ffn_router_w,
           L0_ffn_router_b, L0_ffn_Wi, L0_ffn_Wh, L0_ffn_b, L0_ffn_Wo, L0_ffn_bo):
    import numpy as _np
    import concourse.bacc as _bacc
    from concourse import mybir as _mybir
    from concourse.bass_utils import run_bass_kernel_spmd as _run

    consts = _np.zeros((P, C_COLS), _np.float32)
    consts[:, C_IDENT:C_IDENT + P] = _np.eye(P, dtype=_np.float32)
    q = _np.arange(P)[:, None] % PATCHES
    k = _np.arange(PATCHES)[None, :]
    for w, size in enumerate((9, 17)):
        consts[:, C_BAND + w * PATCHES:C_BAND + (w + 1) * PATCHES] = _np.where(abs(q - k) <= size // 2, 0.0, -BIG)
    odd = (_np.arange(P) // PATCHES) % 2
    for n, scale in enumerate((DH ** -0.5, 1.0, 0.5)):
        consts[:, C_OWN + 2 * n] = (1 - odd) * scale
        consts[:, C_OWN + 2 * n + 1] = odd * scale
    consts[:, C_RANK:C_RANK + EXPERTS] = EXPERTS - _np.arange(EXPERTS)

    a = _np.asarray
    side = 4
    patches = a(x).reshape(IMAGES, 3, side, 16, side, 16).transpose(1, 3, 5, 0, 2, 4).reshape(KCH * P, TOKENS)
    laid = [
        ("patches", patches),
        ("tok_w", a(L0_tok_w).T),
        ("tok_b", a(L0_tok_b).reshape(P, 1)),
        ("qkv_w", a(L0_attn_qkv_w).T),
        ("proj_w", a(L0_attn_proj_w).T),
        ("proj_b", a(L0_attn_proj_b)),
        ("router_w", a(L0_ffn_router_w)),
        ("router_b", a(L0_ffn_router_b)),
        ("w_in", a(L0_ffn_Wi)),
        ("w_hid", a(L0_ffn_Wh)),
        ("gate_b", a(L0_ffn_b)),
        ("w_out", a(L0_ffn_Wo)),
        ("out_b", a(L0_ffn_bo).repeat(TOPK, axis=0)),
        ("consts", consts),
    ]
    nc = _bacc.Bacc("TRN2", target_bir_lowering=False, num_devices=1)
    arrays, args = {}, []
    for name, arr in laid:
        arr = _np.ascontiguousarray(arr)
        arrays[f"in_{name}_dram"] = arr
        args.append(nc.dram_tensor(f"in_{name}_dram", arr.shape, _mybir.dt.from_np(arr.dtype),
                                   kind="ExternalInput").ap())
    args.append(nc.dram_tensor("out_dram", (TOKENS, P), _mybir.dt.float32, kind="ExternalOutput").ap())
    vit_moe_lstm_kernel(nc, *args)
    r = _run(nc, [arrays], core_ids=[0])
    return r.results[0]["out_dram"].reshape(IMAGES, PATCHES, P)
```

```python
from contextlib import ExitStack

import concourse.bass as bass
from concourse import mybir

ALU = mybir.AluOpType
ACT = mybir.ActivationFunctionType
AX_X = mybir.AxisListType.X
F32 = mybir.dt.float32
F16 = mybir.dt.float16
I32 = mybir.dt.int32

P = 128
IMAGES = 128
PATCHES = 16
TOKENS = IMAGES * PATCHES
KCH = 6
HEADS, DH = 8, 16
EXPERTS, TOPK = 8, 2
GATES = 4 * P
ROW_TILES = 4
SUPER = ROW_TILES * P
NSUPER = TOKENS // SUPER
STREAMS = 2
ROUNDS = NSUPER // STREAMS
LN_EPS = 1e-5
RSQRT_GUESS = float(0x5F3759DF)
NEWTON = 3
BIG = 3.0e38
TINY = 2.0 ** -100
W_TOP = 1024.0
EXPONENT = 0x7F800000
TWICE_BIAS = float(254 << 23)
IN_HI, IN_LO, HID_HI, HID_LO = range(4)

SEQ = EXPERTS * TOPK * PATCHES
HALF = SEQ // 2
UNROLL = 4
BODIES = IMAGES // UNROLL

C_IDENT = 0
C_BAND = 128
C_OWN = 160
C_RANK = 166
C_COLS = 174


def vit_moe_lstm_kernel(nc, patches, tok_w, tok_b, qkv_w, proj_w, proj_b, router_w, router_b,
                        w_in, w_hid, gate_b, w_out, out_b, consts, out):
    with ExitStack() as ctx:
        def sb(name, shape, dt=F32):
            return ctx.enter_context(nc.sbuf_tensor(name, shape, dt))

        def sem(name):
            return ctx.enter_context(nc.semaphore(name))

        quads = [ctx.enter_context(nc.psum_tensor(f"quad{z}", [P, 4, 512], F32)) for z in range(2)]
        gate_bank = [[quads[0][:, 2 * g + par, :] for par in range(2)] for g in range(2)]
        turned = [quads[1][:, g, :] for g in range(2)]

        cst = sb("cst", [P, C_COLS])
        ident = cst[:, C_IDENT:C_IDENT + P]
        tokw = sb("tokw", [P, KCH, P])
        tokb = sb("tokb", [P, 1])
        qkvw = sb("qkvw", [P, 3, P])
        projw = sb("projw", [P, P])
        projb = sb("projb", [P, P])
        rw_sb = sb("rw_sb", [P, EXPERTS])
        rb_sb = sb("rb_sb", [P, EXPERTS])
        w16 = sb("w16", [P, EXPERTS, 4, GATES], F16)
        stage = sb("stage", [P, 3, GATES])
        big = sb("big", [P, 2, GATES])
        scl = sb("scl", [P, 10])
        unscale8 = sb("unscale8", [P, EXPERTS])
        unscale = sb("unscale", [P, 2])
        wo = sb("wo", [P, EXPERTS, P])
        bo2 = sb("bo2", [2 * EXPERTS, P])

        h2 = sb("h2", [P, NSUPER * ROW_TILES, P])
        xT = sb("xT", [P, 2, TOKENS], F16)
        maskT = sb("maskT", [2 * SEQ // PATCHES, STREAMS, SUPER], F16)
        ckT = sb("ckT", [2 * SEQ // PATCHES, TOKENS])
        mix = sb("mix", [P, EXPERTS, TOKENS])


        sizes = {"pt": KCH * SUPER, "hT": SUPER, "h1": SUPER, "xn": SUPER, "xnT": SUPER, "qT": SUPER,
                 "kx": 2 * SUPER, "vt": SUPER, "s_a": SUPER, "s_b": SUPER, "s_e": SUPER, "s_p": SUPER,
                 "axT": 2 * SUPER, "oT": SUPER}
        work = sb("work", [P, sum(sizes.values())])
        B = []
        for flat in (work[:, :], mix[:, :, :].rearrange("p e n -> p (e n)")):
            at, one = 0, {}
            for name, size in sizes.items():
                one[name] = flat[:, at:at + size]
                at += size
            one["pt"] = one["pt"].rearrange("p (c n) -> p c n", c=KCH)
            for name in ("h1", "xn", "vt"):
                one[name + "_f"] = one[name]
                one[name] = one[name].rearrange("p (t c) -> p t c", c=P)
            one["ax"] = one["kx"]
            one["kx"] = one["kx"].rearrange("p (h n) -> p h n", h=2)
            B.append(one)
        st = sb("st", [P, STREAMS, 8, 32])
        sti = sb("sti", [P, STREAMS, ROW_TILES], I32)
        bn = sb("bn", [P, STREAMS, ROW_TILES, 6])
        lg = sb("lg", [P, STREAMS, 6, ROW_TILES, EXPERTS])
        ck = sb("ck", [P, STREAMS, ROW_TILES, P])

        xm = sb("xm", [P, 2, 2, SEQ], F16)
        h16 = sb("h16", [P, 2, 2, SEQ], F16)
        hs = sb("hs", [P, 2, SEQ])
        gt = work[:, 0:12 * P].rearrange("p (g n) -> p g n", g=2)
        prod = work[:, 12 * P:16 * P].rearrange("p (g n) -> p g n", g=2)
        thc = sb("thc", [P, 2, P])
        hc = sb("hc", [P, SEQ])
        mst = sb("mst", [P, 2, 2 * SEQ], F16)
        cst_s = work[:, 4 * SUPER:4 * SUPER + 4 * SEQ].rearrange("p (h n) -> p h n", h=2)

        yT = [work[:, z * SUPER:(z + 1) * SUPER] for z in range(2)]

        scr_c = nc.dram_tensor("scr_c", [IMAGES, 16, PATCHES], F32).ap()
        scr_m = nc.dram_tensor("scr_m", [IMAGES, 16, PATCHES], F16).ap()

        names = """const_in w_small_in w_out_in stage_in stage_free diff_ready top_ready prep_done w_ready
            xT_ready zeroed xm_ready ones_ready passed dve_done""".split()
        S = {n: sem(n) for n in names}
        names = """patches_in embedded hT_ready h1_tr h1_ready xn_ready xn_tr xnT_ready qkv_ready q_copied v_copied
            kx_ready scores_ready split_ready shifted exp_ready axT_ready heads_ready oT_ready proj_ready h2_ready
            xn2_ready xn2_tr xn2T_ready xT_hi xT_lo router_ready gap_ready gexp_ready ck_ready ck_tr ckT_ready
            gates_ready ifg_ready o_ready c_ready tr_ready thc_ready h_ready hid_ready low_ready hc_done mixed m_in c_in prod_ready
            scr_stored yT_psum yT_ready y_tr y_ready y_out""".split()
        pair = {n: [sem(f"{n}{z}") for z in range(2)] for n in names}

        block = ctx.enter_context(nc.Block())

        patches_v = patches.rearrange("(c p) n -> p c n", p=P)
        out_v = out.rearrange("(t p) c -> p t c", p=P)

        @block.sync
        def _(sp):
            def load_patches(z, i):
                sp.dma_start(B[z]["pt"], patches_v[:, :, bass.ds((i * STREAMS + z) * SUPER, SUPER)]
                             ).then_inc(pair["patches_in"][z], 16)

            sp.dma_start(tokw[:, :, :], tok_w.rearrange("(c p) n -> p c n", p=P)).then_inc(S["w_small_in"], 16)
            load_patches(0, 0)
            sp.dma_start(tokb[:, :], tok_b).then_inc(S["w_small_in"], 16)
            sp.dma_start(cst[:, :], consts).then_inc(S["const_in"], 16)
            load_patches(1, 0)
            sp.dma_start(qkvw[:, :, :], qkv_w.rearrange("p (t n) -> p t n", t=3)).then_inc(S["w_small_in"], 16)
            sp.dma_start(projw[:, :], proj_w).then_inc(S["w_small_in"], 16)
            sp.dma_start(projb[:, :], proj_b.partition_broadcast(P)).then_inc(S["w_small_in"], 16)
            sp.dma_start(rw_sb[:, :], router_w).then_inc(S["w_small_in"], 16)
            sp.dma_start(rb_sb[:, :], router_b.partition_broadcast(P)).then_inc(S["w_small_in"], 16)
            def load_expert(e):
                for dst, src in ((stage[1:P, 0, :], w_in[bass.ds(e, 1), 1:P, :]),
                                 (stage[0:1, 0, :], gate_b[bass.ds(e, 1), :].unsqueeze(1)),
                                 (stage[:, 1, :], w_hid[bass.ds(e, 1), :, :])):
                    sp.dma_start(dst, src.rearrange("e p n -> (e p) n")).then_inc(S["stage_in"], 16)
                sp.dma_start(stage[1:P, 2, :], w_in[bass.ds(e, 1), 0, :].rearrange("e n -> (e n)")
                             .partition_broadcast(P - 1)).then_inc(S["stage_in"], 16)

            load_expert(0)
            sp.dma_start(wo[:, :, :], w_out.rearrange("e p n -> p e n")).then_inc(S["w_out_in"], 16)
            sp.dma_start(bo2[:, :], out_b).then_inc(S["w_out_in"], 16)
            for z in range(STREAMS):
                sp.wait_ge(pair["embedded"][z], 1)
                load_patches(z, 1)
            with sp.Fori(0, EXPERTS - 1) as e:
                sp.wait_ge(S["stage_free"], e + 1)
                sp.sem_inc(S["passed"])
                load_expert(e + 1)

            with sp.Fori(0, ROUNDS) as i:
                for z in range(STREAMS):
                    n = i * STREAMS + z
                    sp.wait_ge(pair["ckT_ready"][z], i + 2)
                    sp.sem_inc(S["passed"])
                    window = bass.ds(n * SUPER, SUPER)
                    for scr, src in ((scr_c, ckT[0:16, window]), (scr_m, maskT[16:32, z, :])):
                        sp.dma_start(scr[bass.ds(n * 32, 32), :, :].rearrange("s k b -> k s b"),
                                     src.rearrange("k (s b) -> k s b", b=PATCHES)).then_inc(pair["scr_stored"][z], 16)
            for z in range(STREAMS):
                sp.wait_ge(pair["scr_stored"][z], 32 * ROUNDS + 1)

            def load_masks(j, half):
                src = scr_m[bass.ds(j * UNROLL + 2 * half, 2), :, :].rearrange("s k b -> (s k b)")
                sp.dma_start(mst[1:P, half, :], src.partition_broadcast(P - 1)).then_inc(pair["m_in"][half], 16)

            def load_weights(j, half):
                src = scr_c[bass.ds(j * UNROLL + 2 * half, 2), :, :].rearrange("s k b -> (s k b)")
                sp.dma_start(cst_s[:, half, :], src.partition_broadcast(P)).then_inc(pair["c_in"][half], 16)

            for half in range(2):
                load_masks(0, half)
                load_weights(0, half)
            with sp.Fori(0, BODIES - 1) as j:
                sp.wait_ge(S["xm_ready"], j * UNROLL + 2)
                load_masks(j + 1, 0)
                sp.wait_ge(S["xm_ready"], j * UNROLL + 4)
                load_masks(j + 1, 1)
                sp.wait_ge(pair["hc_done"][1], j * UNROLL + 2 + 2)
                sp.sem_inc(S["passed"])
                load_weights(j + 1, 0)
                sp.wait_ge(pair["hc_done"][1], j * UNROLL + 4 + 2)
                sp.sem_inc(S["passed"])
                load_weights(j + 1, 1)
            with sp.Fori(0, ROUNDS) as w:
                for z in range(2):
                    sp.wait_ge(pair["y_ready"][z], w + 2)
                    rows = bass.ds((w * 2 + z) * ROW_TILES, ROW_TILES)
                    sp.dma_start(out_v[:, rows, :], h2[:, rows, :]).then_inc(pair["y_out"][z], 16)
            for z in range(2):
                sp.wait_ge(pair["y_out"][z], 16 * ROUNDS)

        @block.tensor
        def _(pe):
            def tiles(z, bank):
                return [quads[z][:, bank, t * P:(t + 1) * P] for t in range(ROW_TILES)]

            def turn_rows(z, bank, rows, ready):
                for t in range(ROW_TILES):
                    m = pe.transpose(tiles(z, bank)[t], rows[t], ident)
                m.then_inc(pair[ready][z], 1)

            pe.wait_ge(S["w_small_in"], 16 * 7)
            pe.wait_ge(S["const_in"], 16)
            with pe.Fori(0, ROUNDS) as i:
                for z in range(STREAMS):
                    pe.wait_ge(pair["patches_in"][z], (i + 1) * 16)
                    pe.wait_ge(pair["ckT_ready"][z], i + 1)
                    for c in range(KCH):
                        m = pe.matmul(quads[z][:, 0, :], tokw[:, c, :], B[z]["pt"][:, c, :],
                                      start=c == 0, stop=c == KCH - 1)
                    m.then_inc(pair["embedded"][z], 1)
                for z in range(STREAMS):
                    pe.wait_ge(pair["hT_ready"][z], i + 1)
                    turn_rows(z, 1, [B[z]["hT"][:, t * P:(t + 1) * P] for t in range(ROW_TILES)], "h1_tr")
                for z in range(STREAMS):
                    pe.wait_ge(pair["xn_ready"][z], i + 1)
                    turn_rows(z, 2, [B[z]["xn"][:, t, :] for t in range(ROW_TILES)], "xn_tr")
                for z in range(STREAMS):
                    xnT = B[z]["xnT"]
                    pe.wait_ge(pair["xnT_ready"][z], i + 1)
                    pe.matmul(quads[z][:, 0, :], qkvw[:, 0, :], xnT, start=True, stop=True)
                    pe.matmul(quads[z][:, 1, :], qkvw[:, 1, :], xnT, start=True, stop=True)
                    for t in range(ROW_TILES):
                        m = pe.matmul(tiles(z, 3)[t], xnT[:, t * P:(t + 1) * P], qkvw[:, 2, :], start=True, stop=True)
                    m.then_inc(pair["qkv_ready"][z], 1)
                for z in range(STREAMS):
                    qT, kx = B[z]["qT"], B[z]["kx"]
                    pe.wait_ge(pair["q_copied"][z], i + 1)
                    pe.wait_ge(pair["v_copied"][z], i + 1)
                    pe.wait_ge(pair["kx_ready"][z], i + 1)
                    pe.sem_inc(S["passed"])
                    for t in range(ROW_TILES):
                        for c in range(4):
                            for j in range(4):
                                tok = slice(t * P + 32 * j, t * P + 32 * j + 32)
                                m = pe.matmul(quads[z][32 * j:32 * j + 32, c, t * 64:(t + 1) * 64],
                                              qT[32 * c:32 * c + 32, tok], kx[32 * c:32 * c + 32, :, tok],
                                              start=True, stop=True)
                    m.then_inc(pair["scores_ready"][z], 1)
                for z in range(STREAMS):
                    vt, axT = B[z]["vt"], B[z]["axT"].rearrange("p (r q) -> p r q", q=32)
                    pe.wait_ge(pair["axT_ready"][z], i + 1)
                    pe.sem_inc(S["passed"])
                    for t in range(ROW_TILES):
                        for j in range(4):
                            for c in range(4):
                                b0 = c * 8 + t * 2
                                m = pe.matmul(quads[z][32 * c:32 * c + 32, j, t * 64:(t + 1) * 64],
                                              vt[32 * j:32 * j + 32, t, 32 * c:32 * c + 32],
                                              axT[32 * j:32 * j + 32, b0:b0 + 2, :], start=True, stop=True)
                    m.then_inc(pair["heads_ready"][z], 1)
                for z in range(STREAMS):
                    pe.wait_ge(pair["oT_ready"][z], i + 1)
                    for t in range(ROW_TILES):
                        m = pe.matmul(tiles(z, 0)[t], B[z]["oT"][:, t * P:(t + 1) * P], projw[:, :],
                                      start=True, stop=True)
                    m.then_inc(pair["proj_ready"][z], 1)
                for z in range(STREAMS):
                    pe.wait_ge(pair["xn2_ready"][z], i + 1)
                    turn_rows(z, 1, [B[z]["xn"][:, t, :] for t in range(ROW_TILES)], "xn2_tr")
                for z in range(STREAMS):
                    pe.wait_ge(pair["xn2T_ready"][z], i + 1)
                    for t in range(ROW_TILES):
                        m = pe.matmul(quads[z][:, 2, t * EXPERTS:(t + 1) * EXPERTS],
                                      B[z]["xnT"][:, t * P:(t + 1) * P], rw_sb[:, :], start=True, stop=True)
                    m.then_inc(pair["router_ready"][z], 1)
                for z in range(STREAMS):
                    pe.wait_ge(pair["ck_ready"][z], i + 1)
                    turn_rows(z, 3, [ck[:, z, t, :] for t in range(ROW_TILES)], "ck_tr")

            def gates(g, par):
                return gate_bank[g][par]

            def from_inputs(g, s, par, passes=range(3)):
                pe.wait_ge(S["xm_ready"], s + 1)
                for n in passes:
                    part, w = ((0, IN_HI), (0, IN_LO), (1, IN_HI))[n]
                    for q in range(4):
                        e = 4 * g + q
                        pe.matmul(gates(g, par)[32 * q:32 * q + 32], xm[:, par, part, 32 * e:32 * e + 32],
                                  w16[:, e, w, :], start=n == 0, stop=False)

            def from_hidden(g, s, par, passes=range(3)):
                for n in passes:
                    part, w = ((0, HID_HI), (0, HID_LO), (1, HID_HI))[n]
                    if n == 0:
                        pe.wait_ge(pair["h_ready"][g], s + 1)
                    if n == 2:
                        pe.wait_ge(pair["low_ready"][g], s + 1)
                    for q in range(4):
                        e = 4 * g + q
                        m = pe.matmul(gates(g, par)[32 * q:32 * q + 32], h16[:, 1 - par, part, 32 * e:32 * e + 32],
                                      w16[:, e, w, :], start=False, stop=n == 2)
                if n == 2:
                    m.then_inc(pair["gates_ready"][g], 1)

            def turn(g, s):
                pe.wait_ge(pair["o_ready"][g], s + 1)
                pe.transpose(turned[g][:, 0:P], gt[:, g, 3 * P:4 * P], ident)
                pe.wait_ge(pair["c_ready"][g], s + 1)
                pe.transpose(turned[g][:, P:2 * P], gt[:, g, 4 * P:5 * P], ident).then_inc(pair["tr_ready"][g], 1)

            pe.wait_ge(S["w_ready"], 1)
            pe.wait_ge(S["zeroed"], 1)
            for z in range(STREAMS):
                pe.wait_ge(pair["ckT_ready"][z], ROUNDS + 1)
            from_inputs(0, 0, 0)
            from_inputs(1, 0, 0)
            from_hidden(0, 0, 0)

            def steps(base, last):
                for u in range(UNROLL):
                    s, par = base + u, u % 2
                    end = last and u == UNROLL - 1
                    if not end:
                        from_inputs(0, s + 1, 1 - par, (0, 1))
                    from_hidden(1, s, par)
                    if not end:
                        from_inputs(0, s + 1, 1 - par, (2,))
                    turn(0, s)
                    if not end:
                        from_inputs(1, s + 1, 1 - par)
                        from_hidden(0, s + 1, 1 - par, (0,))
                    turn(1, s)
                    if not end:
                        from_hidden(0, s + 1, 1 - par, (1, 2))

            with pe.Fori(0, BODIES - 1) as j:
                steps(j * UNROLL, False)
            steps((BODIES - 1) * UNROLL, True)

            pe.wait_ge(pair["y_ready"][0], 1)
            pe.wait_ge(pair["y_ready"][1], 1)
            with pe.Fori(0, ROUNDS) as w:
                for z in range(2):
                    window = bass.ds((w * 2 + z) * SUPER, SUPER)
                    for e in range(EXPERTS):
                        pe.matmul(quads[0][:, z, :], wo[:, e, :], mix[:, e, window], start=e == 0, stop=False)
                    pe.matmul(quads[0][:, z, :], bo2[:, :], ckT[0:2 * EXPERTS, window],
                              start=False, stop=True).then_inc(pair["yT_psum"][z], 1)
                for z in range(2):
                    pe.wait_ge(pair["yT_ready"][z], w + 1)
                    pe.wait_ge(pair["y_ready"][z], w + 1)
                    for t in range(ROW_TILES):
                        m = pe.transpose(quads[1][:, z, t * P:(t + 1) * P], yT[z][:, t * P:(t + 1) * P], ident)
                    m.then_inc(pair["y_tr"][z], 1)

        @block.scalar
        def _(act):
            def copy(z, i, after, dst, bank, ready):
                act.wait_ge(pair[after][z], i + 1)
                act.activation(dst, quads[z][:, bank, :], ACT.Copy).then_inc(pair[ready][z], 1)

            def own_head(z, dst, src, n, scale=C_OWN):
                return act.activation(dst, src, ACT.Identity, scale=cst[:, scale + n:scale + n + 1])

            act.wait_ge(S["w_small_in"], 16 * 7)
            act.wait_ge(S["const_in"], 16)
            with act.Fori(0, ROUNDS) as i:
                for z in range(STREAMS):
                    act.wait_ge(pair["embedded"][z], i + 1)
                    act.activation(B[z]["hT"], quads[z][:, 0, :], ACT.Identity, bias=tokb[:, 0:1]
                                   ).then_inc(pair["hT_ready"][z], 1)
                for z in range(STREAMS):
                    copy(z, i, "h1_tr", B[z]["h1_f"], 1, "h1_ready")
                for z in range(STREAMS):
                    copy(z, i, "xn_tr", B[z]["xnT"], 2, "xnT_ready")
                for z in range(STREAMS):
                    act.wait_ge(pair["qkv_ready"][z], i + 1)
                    own_head(z, B[z]["kx"][:, 0, :], quads[z][:, 1, :], 0)
                    own_head(z, B[z]["kx"][:, 1, :], quads[z][:, 1, :], 1).then_inc(pair["kx_ready"][z], 1)
                    copy(z, i, "qkv_ready", B[z]["qT"], 0, "q_copied")
                    copy(z, i, "qkv_ready", B[z]["vt_f"], 3, "v_copied")
                for z in range(STREAMS):
                    act.wait_ge(pair["scores_ready"][z], i + 1)
                    s_all = quads[z][:, :, 0:256].rearrange("p c (r i k) -> p c r i k", i=2, k=PATCHES)
                    for n, dst in enumerate(("s_b", "s_e")):
                        ins = own_head(z, B[z][dst].rearrange("p (c r k) -> p c r k", c=4, k=PATCHES),
                                       s_all[:, :, :, n, :], n + 2)
                    ins.then_inc(pair["split_ready"][z], 1)
                for w in range(2):
                    for z in range(STREAMS):
                        act.wait_ge(pair["shifted"][z], i * 2 + (w + 1))
                        act.activation(B[z]["s_e"], B[z]["s_b"], ACT.Exp).then_inc(pair["exp_ready"][z], 1)
                for z in range(STREAMS):
                    act.wait_ge(pair["h2_ready"][z], i + 1)
                    act.activation(h2[:, bass.ds((i * STREAMS + z) * ROW_TILES, ROW_TILES), :], B[z]["h1"], ACT.Copy)
                    copy(z, i, "xn2_tr", B[z]["xnT"], 1, "xn2T_ready")
                    act.wait_ge(pair["xn2T_ready"][z], i + 1)
                    act.activation(xT[:, 0, bass.ds((i * STREAMS + z) * SUPER, SUPER)], B[z]["xnT"], ACT.Copy
                                   ).then_inc(pair["xT_hi"][z], 1)
                for z in range(STREAMS):
                    act.wait_ge(pair["gap_ready"][z], i + 1)
                    act.activation(st[:, z, 7, 0:4], st[:, z, 6, 0:4], ACT.Exp).then_inc(pair["gexp_ready"][z], 1)
                for z in range(STREAMS):
                    act.wait_ge(pair["ck_tr"][z], i + 1)
                    act.wait_ge(pair["scr_stored"][z], i * 32 + 1)
                    act.activation(maskT[:, z, :], quads[z][0:32, 3, :], ACT.Copy)
                    act.activation(ckT[:, bass.ds((i * STREAMS + z) * SUPER, SUPER)], quads[z][0:32, 3, :], ACT.Copy
                                   ).then_inc(pair["ckT_ready"][z], 1)

            def gate_tanh(g, s, par, gates, ready):
                if ready == "ifg_ready":
                    act.wait_ge(pair["gates_ready"][g], s + 1)
                act.activation(gt[:, g, gates], gate_bank[g][par][:, gates], ACT.Tanh, scale=unscale[:, g:g + 1]
                               ).then_inc(pair[ready][g], 1)

            def cell_tanh(g, s):
                act.wait_ge(pair["tr_ready"][g], s + 1)
                act.activation(thc[:, g, :], turned[g][:, P:2 * P], ACT.Tanh, scale=0.5
                               ).then_inc(pair["thc_ready"][g], 1)

            IFG, O = slice(0, 3 * P), slice(3 * P, 4 * P)
            act.wait_ge(S["w_ready"], 1)
            gate_tanh(0, 0, 0, IFG, "ifg_ready")

            def steps(base, last):
                for u in range(UNROLL):
                    s, par = base + u, u % 2
                    gate_tanh(0, s, par, O, "o_ready")
                    gate_tanh(1, s, par, IFG, "ifg_ready")
                    cell_tanh(0, s)
                    gate_tanh(1, s, par, O, "o_ready")
                    cell_tanh(1, s)
                    if not (last and u == UNROLL - 1):
                        gate_tanh(0, s + 1, 1 - par, IFG, "ifg_ready")

            with act.Fori(0, BODIES - 1) as j:
                steps(j * UNROLL, False)
            steps((BODIES - 1) * UNROLL, True)
            with act.Fori(0, ROUNDS) as w:
                for z in range(2):
                    act.wait_ge(pair["yT_psum"][z], w + 1)
                    act.activation(yT[z], quads[0][:, z, :], ACT.Copy).then_inc(pair["yT_ready"][z], 1)

        @block.vector
        def _(dve):
            for z in range(STREAMS):
                dve.memset(ck[:, z, :, :], 0.0).then_inc(pair["ckT_ready"][z], 1)
                dve.memset(st[:, z, 0, :], 0.0).then_inc(pair["scr_stored"][z], 1)
            for z in range(STREAMS):
                dve.wait_ge(pair["ckT_ready"][z], 1)
                dve.wait_ge(pair["scr_stored"][z], 1)

            LINKS = 200
            dve.wait_ge(S["const_in"], 16)
            dve.wait_ge(S["w_small_in"], 16 * 7)
            with dve.Fori(0, ROUNDS) as i:
                count, last = [0], [None, None]

                def both(op, after=None, times=(1, 1), ready=None):
                    for z in range(STREAMS):
                        if last[z] is not None:
                            done, per_round, n = last[z]
                            dve.wait_ge(done, i * per_round + n)
                        if after is not None:
                            dve.wait_ge(pair[after][z], i * times[0] + times[1])
                        ins = op(z)
                        if ready is not None:
                            last[z] = (pair[ready][z], times[0], times[1])
                            ins.then_inc(pair[ready][z], 1)
                        else:
                            count[0] += 1
                            last[z] = (S["dve_done"], LINKS, count[0])
                            ins.then_inc(S["dve_done"], 1)

                def tt(out, a, b, op):
                    return dve.tensor_tensor(out, a, b, op)

                def ts(out, a, s1, s2, op0, op1=None):
                    if op1 is None:
                        return dve.tensor_scalar(out, a, s1, None, op0)
                    return dve.tensor_scalar(out, a, s1, s2, op0, op1)

                def stt(out, a, s1, b, op0, op1):
                    return dve.scalar_tensor_tensor(out=out, in0=a, scalar=s1, in1=b, op0=op0, op1=op1)

                def small(z, n, width=ROW_TILES):
                    return st[:, z, n, 0:width]

                def layernorm(src, after, ready):
                    for t in range(ROW_TILES):
                        both(lambda z: dve.bn_stats(bn[:, z, t, :], B[z][src][:, t, :]), after if t == 0 else None)
                    even, odd = (lambda z: bn[:, z, :, 1]), (lambda z: bn[:, z, :, 4])
                    both(lambda z: tt(small(z, 0), even(z), odd(z), ALU.add))
                    both(lambda z: tt(small(z, 1), even(z), odd(z), ALU.subtract))
                    both(lambda z: tt(small(z, 2), bn[:, z, :, 2], bn[:, z, :, 5], ALU.add))
                    both(lambda z: ts(small(z, 2), small(z, 2), 1.0 / P, LN_EPS, ALU.mult, ALU.add))
                    both(lambda z: stt(small(z, 1), small(z, 1), 0.25, small(z, 1), ALU.mult, ALU.mult))
                    both(lambda z: ts(small(z, 0), small(z, 0), 0.5, None, ALU.mult))
                    both(lambda z: tt(small(z, 3), small(z, 1), small(z, 2), ALU.add))
                    both(lambda z: ts(sti[:, z, :], small(z, 3).bitcast(I32), 1, None, ALU.logical_shift_right))
                    both(lambda z: ts(small(z, 4).bitcast(I32), sti[:, z, :], -1.0, RSQRT_GUESS, ALU.mult, ALU.add))
                    for _ in range(NEWTON):
                        both(lambda z: stt(small(z, 5), small(z, 4), -0.5, small(z, 4), ALU.mult, ALU.mult))
                        both(lambda z: tt(small(z, 5), small(z, 5), small(z, 3), ALU.mult))
                        both(lambda z: stt(small(z, 4), small(z, 5), 1.5, small(z, 4), ALU.add, ALU.mult))
                    for t in range(ROW_TILES):
                        both(lambda z: ts(B[z]["xn"][:, t, :], B[z][src][:, t, :], st[:, z, 0, t:t + 1],
                                          st[:, z, 4, t:t + 1], ALU.subtract, ALU.mult),
                             ready=ready if t == ROW_TILES - 1 else None)

                def keys(a):
                    return a.rearrange("p (r k) -> p r k", k=PATCHES)

                def per_row(z, n):
                    return small(z, n, 32).unsqueeze(2).to_broadcast([P, 32, PATCHES])

                def own_col(n):
                    return cst[:, C_OWN + n:C_OWN + n + 1]

                def weights_top(n):
                    dve.wait_ge(S["diff_ready"], i * 4 + (n + 1))
                    power, minus_inverse = scl[:, 0:1], scl[:, 1:2]
                    chain = (lambda: stt(big[:, :, :], stage[:, 0:2, :], -1.0, stage[:, 0:2, :], ALU.mult, ALU.max),
                             lambda: dve.tensor_reduce(scl[:, 8:9], big[:, :, :].rearrange("p a n -> p (a n)"), AX_X, ALU.max),
                             lambda: ts(scl[:, 8:9], scl[:, 8:9], TINY, None, ALU.max),
                             lambda: ts(power.bitcast(I32), scl[:, 8:9].bitcast(I32), EXPONENT, None,
                                        ALU.bitwise_and),
                             lambda: ts(scl[:, 8:9].bitcast(I32), power.bitcast(I32), -1.0, TWICE_BIAS, ALU.mult,
                                        ALU.add),
                             lambda: ts(minus_inverse, scl[:, 8:9], -1.0, None, ALU.mult))
                    for m, op in enumerate(chain):
                        if m < len(chain) - 1:
                            count[0] += 1
                            op().then_inc(S["dve_done"], 1)
                            dve.wait_ge(S["dve_done"], i * LINKS + count[0])
                        else:
                            op().then_inc(S["top_ready"], 1)

                weights_top(0)
                layernorm("h1", "h1_ready", "xn_ready")
                both(lambda z: tt(B[z]["h1"], B[z]["h1"], projb[:, :].unsqueeze(1).to_broadcast([P, ROW_TILES, P]),
                                  ALU.add))
                weights_top(1)
                both(lambda z: tt(B[z]["s_a"], B[z]["s_b"], B[z]["s_e"], ALU.add), "split_ready")
                for w in range(2):
                    band = cst[:, C_BAND + w * PATCHES:C_BAND + (w + 1) * PATCHES] \
                        .unsqueeze(1).to_broadcast([P, 32, PATCHES])
                    both(lambda z: tt(keys(B[z]["s_b"]), keys(B[z]["s_a"]), band, ALU.add))
                    both(lambda z: dve.tensor_reduce(small(z, 0, 32), keys(B[z]["s_b"]), AX_X, ALU.max))
                    both(lambda z: tt(keys(B[z]["s_b"]), keys(B[z]["s_b"]), per_row(z, 0), ALU.subtract),
                         None, (2, w + 1), "shifted")
                    both(lambda z: dve.tensor_reduce(small(z, 1, 32), keys(B[z]["s_e"]), AX_X, ALU.add),
                         "exp_ready", (2, w + 1))
                    both(lambda z: dve.reciprocal(small(z, 2, 32), small(z, 1, 32)))
                    dst = "s_p" if w == 0 else "s_e"
                    both(lambda z: tt(keys(B[z][dst]), keys(B[z]["s_e"]), per_row(z, 2), ALU.mult))
                both(lambda z: tt(B[z]["s_p"], B[z]["s_p"], B[z]["s_e"], ALU.add))
                for h in range(2):
                    both(lambda z: ts(B[z]["ax"].rearrange("p (r k) -> p r k", k=32)
                                      [:, :, h * PATCHES:(h + 1) * PATCHES], keys(B[z]["s_p"]), own_col(2 + h),
                                      None, ALU.mult))
                both(lambda z: dve.transpose(B[z]["axT"], B[z]["ax"]), ready="axT_ready")
                weights_top(2)
                for j in range(4):
                    def parts(z):
                        return (quads[z][:, j, 0:256].rearrange("p (t h q) -> p t h q", t=4, h=2),
                                B[z]["oT"].rearrange("p (t j q) -> p t j q", t=4, j=4)[:, :, j, :])
                    both(lambda z: ts(parts(z)[1], parts(z)[0][:, :, 0, :], own_col(4), None, ALU.mult),
                         "heads_ready" if j == 0 else None)
                    both(lambda z: stt(parts(z)[1], parts(z)[0][:, :, 1, :], own_col(5), parts(z)[1],
                                       ALU.mult, ALU.add), ready="oT_ready" if j == 3 else None)
                both(lambda z: tt(B[z]["h1_f"], B[z]["h1_f"], quads[z][:, 0, :], ALU.add), "proj_ready",
                     ready="h2_ready")
                layernorm("h1", "h2_ready", "xn2_ready")
                weights_top(3)
                for_all = lambda z: bass.ds((i * STREAMS + z) * SUPER, SUPER)
                both(lambda z: tt(xT[:, 1, for_all(z)], B[z]["xnT"], xT[:, 0, for_all(z)], ALU.subtract), "xT_hi",
                     ready="xT_lo")
                rank = cst[:, C_RANK:C_RANK + EXPERTS].unsqueeze(1).to_broadcast([P, ROW_TILES, EXPERTS])
                router_bias = rb_sb[:, :].unsqueeze(1).to_broadcast([P, ROW_TILES, EXPERTS])
                LOGITS, SCORE, FIRST, SECOND, REST, EQUAL = range(6)

                def cols(z, n):
                    return small(z, n).unsqueeze(2).to_broadcast([P, ROW_TILES, EXPERTS])

                both(lambda z: tt(lg[:, z, LOGITS], quads[z][:, 2, 0:32].rearrange("p (t e) -> p t e", e=EXPERTS),
                                  router_bias, ALU.add), "router_ready")
                for n, (src, hot) in enumerate(((LOGITS, FIRST), (REST, SECOND))):
                    both(lambda z: dve.tensor_reduce(small(z, n), lg[:, z, src], AX_X, ALU.max))
                    both(lambda z: tt(lg[:, z, EQUAL], lg[:, z, src], cols(z, n), ALU.is_equal))
                    both(lambda z: tt(lg[:, z, SCORE], lg[:, z, EQUAL], rank, ALU.mult))
                    both(lambda z: dve.tensor_reduce(small(z, 2), lg[:, z, SCORE], AX_X, ALU.max))
                    both(lambda z: tt(lg[:, z, hot], lg[:, z, SCORE], cols(z, 2), ALU.is_equal))
                    if n == 0:
                        both(lambda z: stt(lg[:, z, REST], lg[:, z, FIRST], -BIG, lg[:, z, LOGITS],
                                           ALU.mult, ALU.add))
                both(lambda z: tt(small(z, 6), small(z, 1), small(z, 0), ALU.subtract), ready="gap_ready")
                both(lambda z: ts(small(z, 3), small(z, 7), 1.0, None, ALU.add), "gexp_ready")
                both(lambda z: dve.reciprocal(small(z, 4), small(z, 3)))
                both(lambda z: tt(small(z, 5), small(z, 7), small(z, 4), ALU.mult))
                for k, hot in enumerate((FIRST, SECOND)):
                    def choice(z, rows):
                        return ck[:, z, :, rows:rows + 16].rearrange("p t (e k) -> p t e k", k=2)[:, :, :, k]
                    both(lambda z: stt(choice(z, 0), lg[:, z, hot], 0.5, cols(z, 4 + k), ALU.mult, ALU.mult))
                    both(lambda z: dve.tensor_copy(choice(z, 16), lg[:, z, hot]), ready="ck_ready" if k else None)
                assert count[0] == LINKS, count[0]

            for z in range(STREAMS):
                dve.wait_ge(pair["xT_lo"][z], ROUNDS)
            dve.memset(xT[0:1, 0, :], 1.0).then_inc(S["xT_ready"], 1)
            dve.memset(xT[0:1, 1, :], 0.0).then_inc(S["xT_ready"], 1)
            dve.memset(gt[:, :, 4 * P:], 0.0).then_inc(S["zeroed"], 1)
            dve.memset(h16[:, :, 0, 0:HALF], 0.0).then_inc(pair["h_ready"][0], 1)
            dve.memset(h16[:, :, 0, HALF:], 0.0).then_inc(pair["h_ready"][1], 1)
            for g in range(2):
                dve.memset(h16[:, :, 1, g * HALF:(g + 1) * HALF], 0.0).then_inc(pair["low_ready"][g], 1)
            dve.wait_ge(S["zeroed"], 1)
            for g in range(2):
                dve.wait_ge(pair["h_ready"][g], 1)
                dve.wait_ge(pair["low_ready"][g], 1)

            def products(g, s):
                dve.wait_ge(pair["ifg_ready"][g], s + 1)
                dve.scalar_tensor_tensor(out=prod[:, g, :].rearrange("p (a u) -> p a u", u=P),
                                         in0=gt[:, g, 0:2 * P].rearrange("p (a u) -> p a u", u=P), scalar=1.0,
                                         in1=gt[:, g, 2 * P:].rearrange("p (a u) -> p a u", a=2)[:, :, 0:P],
                                         op0=ALU.add, op1=ALU.mult).then_inc(pair["prod_ready"][g], 1)

            def cell(g, s):
                dve.wait_ge(pair["prod_ready"][g], s + 1)
                dve.scalar_tensor_tensor(out=gt[:, g, 4 * P:5 * P], in0=prod[:, g, P:], scalar=0.5,
                                         in1=prod[:, g, 0:P], op0=ALU.mult, op1=ALU.add
                                         ).then_inc(pair["c_ready"][g], 1)

            def cols(g):
                return slice(g * HALF, (g + 1) * HALF)

            def hidden_high(g, s, par):
                dve.wait_ge(pair["thc_ready"][g], s + 1)
                dve.scalar_tensor_tensor(out=h16[:, par, 0, cols(g)], in0=turned[g][:, 0:P], scalar=1.0,
                                         in1=thc[:, g, :], op0=ALU.add, op1=ALU.mult
                                         ).then_inc(pair["h_ready"][g], 1)

            def hidden_low(g, s, par):
                dve.wait_ge(pair["hc_done"][g], s + 1)
                dve.scalar_tensor_tensor(out=hs[:, par, cols(g)], in0=turned[g][:, 0:P], scalar=1.0,
                                         in1=thc[:, g, :], op0=ALU.add, op1=ALU.mult
                                         ).then_inc(pair["hid_ready"][g], 1)
                dve.wait_ge(pair["h_ready"][g], s + 2)
                dve.wait_ge(pair["hid_ready"][g], s + 1)
                dve.tensor_tensor(h16[:, par, 1, cols(g)], hs[:, par, cols(g)], h16[:, par, 0, cols(g)],
                                  ALU.subtract).then_inc(pair["low_ready"][g], 1)

            def masked_input(s, par, half, in_half, count):
                dve.wait_ge(pair["m_in"][half], count)
                x_s = xT[:, :, bass.ds(s * PATCHES, PATCHES)].unsqueeze(2).to_broadcast([P, 2, 16, PATCHES])
                m_s = mst[:, half, in_half * SEQ:(in_half + 1) * SEQ].unsqueeze(1).to_broadcast([P, 2, SEQ])
                dve.tensor_tensor(xm[:, par, :, :].rearrange("p a (k b) -> p a k b", b=PATCHES), x_s,
                                   m_s.rearrange("p a (k b) -> p a k b", b=PATCHES), ALU.mult
                                   ).then_inc(S["xm_ready"], 1)

            dve.wait_ge(S["xT_ready"], 2)
            dve.wait_ge(S["ones_ready"], 5)
            masked_input(0, 0, 0, 0, 16)
            masked_input(1, 1, 0, 1, 16)
            products(0, 0)
            cell(0, 0)

            def steps(j, last):
                for u in range(UNROLL):
                    s, par = j * UNROLL + u, u % 2
                    if u < 2 or not last:
                        masked_input(s + 2, par, (u // 2 + 1) % 2, par, j * 16 + (16 if u < 2 else 32))
                    products(1, s)
                    hidden_high(0, s, par)
                    cell(1, s)
                    hidden_low(0, s, par)
                    hidden_high(1, s, par)
                    hidden_low(1, s, par)
                    if not (last and u == UNROLL - 1):
                        products(0, s + 1)
                        cell(0, s + 1)

            with dve.Fori(0, BODIES - 1) as j:
                steps(j, False)
            steps(BODIES - 1, True)

            with dve.Fori(0, ROUNDS) as w:
                for z in range(2):
                    dve.wait_ge(pair["y_tr"][z], w + 1)
                    rows = h2[:, bass.ds((w * 2 + z) * ROW_TILES, ROW_TILES), :]
                    dve.tensor_tensor(rows, quads[1][:, z, :].rearrange("p (t c) -> p t c", c=P), rows, ALU.add
                                      ).then_inc(pair["y_ready"][z], 1)

        @block.gpsimd
        def _(pool):
            for g in range(2):
                pool.memset(hs[:, g, :], 0.0).then_inc(pair["hc_done"][g], 2)
                pool.memset(hc[:, g * HALF:(g + 1) * HALF], 0.0).then_inc(pair["mixed"][g], 1)
            pool.memset(mst[0:1, :, :], 1.0).then_inc(S["ones_ready"], 1)
            pool.memset(scl[:, 7:8], 1.0 / W_TOP).then_inc(S["ones_ready"], 1)
            pool.memset(scl[:, 6:7], -W_TOP).then_inc(S["ones_ready"], 1)
            pool.memset(stage[0:1, 2, :], 0.0).then_inc(S["ones_ready"], 1)
            pool.memset(scl[:, 9:10], 0.0).then_inc(S["ones_ready"], 1)
            pool.wait_ge(S["ones_ready"], 5)
            STEPS = 9
            with pool.Fori(0, EXPERTS) as e:
                count = [0]

                def step(ins):
                    count[0] += 1
                    ins.then_inc(S["prep_done"], 1)
                    pool.wait_ge(S["prep_done"], e * STEPS + count[0])
                    pool.sem_inc(S["passed"])

                pool.wait_ge(S["stage_in"], (e + 1) * 64)
                pool.sem_inc(S["passed"])
                both, top = stage[:, 0:2, :], [scl[:, n:n + 1] for n in range(8)]
                zero2 = scl[:, 9:10].unsqueeze(2).to_broadcast([P, 2, GATES])
                step(pool.tensor_tensor(stage[:, 0, :], stage[:, 0, :], stage[:, 2, :], ALU.subtract))
                pool.sem_inc(S["diff_ready"])
                pool.wait_ge(S["top_ready"], e + 1)
                pool.sem_inc(S["passed"])
                step(pool.partition_all_reduce(scl[:, 2:4], scl[:, 0:2], P, bass.bass_isa.ReduceOp.max))
                step(pool.tensor_tensor(unscale8[:, bass.ds(e, 1)], top[2], top[7], ALU.mult))
                step(pool.tensor_tensor(top[5], top[6], top[3], ALU.mult))
                step(pool.tensor_scalar(stage[:, 0, :], stage[:, 0, :], top[5], 0.5, ALU.mult, ALU.mult))
                step(pool.tensor_scalar(stage[:, 1, :], stage[:, 1, :], top[5], 0.25, ALU.mult, ALU.mult))
                cell_gate = stage[:, 0:2, 2 * P:3 * P]
                step(pool.tensor_scalar(cell_gate, cell_gate, 2.0, None, ALU.mult))
                high, low = (w16[:, bass.ds(e, 1), n::2, :].rearrange("p e a n -> p (e a) n") for n in range(2))
                step(pool.tensor_tensor(high, both, zero2, ALU.add))
                step(pool.tensor_tensor(low, both, high, ALU.subtract))
                pool.sem_inc(S["stage_free"])
                assert count[0] == STEPS
            for e in range(EXPERTS):
                q = slice(32 * (e % 4), 32 * (e % 4) + 32)
                pool.tensor_copy(unscale[q, e // 4:e // 4 + 1], unscale8[q, e:e + 1]).then_inc(S["ones_ready"], 1)
            pool.wait_ge(S["w_out_in"], 32)
            pool.tensor_scalar(bo2[:, :], bo2[:, :], 2.0, None, ALU.mult).then_inc(S["ones_ready"], 1)
            pool.wait_ge(S["ones_ready"], 5 + EXPERTS + 1)
            pool.memset(scl[:, 0:1], 0.0).then_inc(S["w_ready"], 1)

            def weighted_state(g, s, par, half, in_half, count):
                cols = slice(g * HALF, (g + 1) * HALF)
                if g == 0:
                    pool.wait_ge(pair["c_in"][half], count)
                pool.wait_ge(pair["hid_ready"][g], s + 1)
                pool.wait_ge(pair["mixed"][g], s + 1)
                pool.tensor_tensor(hc[:, cols], hs[:, par, cols],
                                   cst_s[:, half, in_half * SEQ + g * HALF:in_half * SEQ + (g + 1) * HALF],
                                   ALU.mult).then_inc(pair["hc_done"][g], 1)
                pool.wait_ge(pair["hc_done"][g], s + 1 + 2)
                by_choice = hc[:, cols].rearrange("p (e k b) -> p e k b", k=2, b=PATCHES)
                pool.tensor_tensor(mix[:, 4 * g:4 * g + 4, bass.ds(s * PATCHES, PATCHES)], by_choice[:, :, 0, :],
                                   by_choice[:, :, 1, :], ALU.add).then_inc(pair["mixed"][g], 1)

            def steps(j, last):
                for u in range(UNROLL):
                    s, par = j * UNROLL + u, u % 2
                    for g in range(2):
                        weighted_state(g, s, par, u // 2, par, j * 16 + 16)

            with pool.Fori(0, BODIES - 1) as j:
                steps(j, False)
            steps(BODIES - 1, True)
            for g in range(2):
                pool.wait_ge(pair["mixed"][g], IMAGES + 1)
            for z in range(2):
                pool.memset(hc[:, z * P:(z + 1) * P], 0.0).then_inc(pair["y_ready"][z], 1)


def kernel(x, L0_tok_w, L0_tok_b, L0_attn_qkv_w, L0_attn_proj_w, L0_attn_proj_b, L0_ffn_router_w,
           L0_ffn_router_b, L0_ffn_Wi, L0_ffn_Wh, L0_ffn_b, L0_ffn_Wo, L0_ffn_bo):
    import numpy as _np
    import concourse.bacc as _bacc
    from concourse import mybir as _mybir
    from concourse.bass_utils import run_bass_kernel_spmd as _run

    consts = _np.zeros((P, C_COLS), _np.float32)
    consts[:, C_IDENT:C_IDENT + P] = _np.eye(P, dtype=_np.float32)
    q = _np.arange(P)[:, None] % PATCHES
    k = _np.arange(PATCHES)[None, :]
    for w, size in enumerate((9, 17)):
        consts[:, C_BAND + w * PATCHES:C_BAND + (w + 1) * PATCHES] = _np.where(abs(q - k) <= size // 2, 0.0, -BIG)
    odd = (_np.arange(P) // PATCHES) % 2
    for n, scale in enumerate((DH ** -0.5, 1.0, 0.5)):
        consts[:, C_OWN + 2 * n] = (1 - odd) * scale
        consts[:, C_OWN + 2 * n + 1] = odd * scale
    consts[:, C_RANK:C_RANK + EXPERTS] = EXPERTS - _np.arange(EXPERTS)

    a = _np.asarray
    side = 4
    patches = a(x).reshape(IMAGES, 3, side, 16, side, 16).transpose(1, 3, 5, 0, 2, 4).reshape(KCH * P, TOKENS)
    laid = [
        ("patches", patches),
        ("tok_w", a(L0_tok_w).T),
        ("tok_b", a(L0_tok_b).reshape(P, 1)),
        ("qkv_w", a(L0_attn_qkv_w).T),
        ("proj_w", a(L0_attn_proj_w).T),
        ("proj_b", a(L0_attn_proj_b)),
        ("router_w", a(L0_ffn_router_w)),
        ("router_b", a(L0_ffn_router_b)),
        ("w_in", a(L0_ffn_Wi)),
        ("w_hid", a(L0_ffn_Wh)),
        ("gate_b", a(L0_ffn_b)),
        ("w_out", a(L0_ffn_Wo)),
        ("out_b", a(L0_ffn_bo).repeat(TOPK, axis=0)),
        ("consts", consts),
    ]
    nc = _bacc.Bacc("TRN2", target_bir_lowering=False, num_devices=1)
    arrays, args = {}, []
    for name, arr in laid:
        arr = _np.ascontiguousarray(arr)
        arrays[f"in_{name}_dram"] = arr
        args.append(nc.dram_tensor(f"in_{name}_dram", arr.shape, _mybir.dt.from_np(arr.dtype),
                                   kind="ExternalInput").ap())
    args.append(nc.dram_tensor("out_dram", (TOKENS, P), _mybir.dt.float32, kind="ExternalOutput").ap())
    vit_moe_lstm_kernel(nc, *args)
    r = _run(nc, [arrays], core_ids=[0])
    return r.results[0]["out_dram"].reshape(IMAGES, PATCHES, P)
```

```python
from contextlib import ExitStack

import concourse.bass as bass
from concourse import mybir

ALU = mybir.AluOpType
ACT = mybir.ActivationFunctionType
AX_X = mybir.AxisListType.X
F32 = mybir.dt.float32
F16 = mybir.dt.float16
I32 = mybir.dt.int32

P = 128
IMAGES = 128
PATCHES = 16
TOKENS = IMAGES * PATCHES
KCH = 6
DH = 16
EXPERTS, TOPK = 8, 2
GATES = 4 * P
ROW_TILES = 4
SUPER = ROW_TILES * P
NSUPER = TOKENS // SUPER
TILES = NSUPER * ROW_TILES
STREAMS = 2
ROUNDS = NSUPER // STREAMS
LN_EPS = 1e-5
RSQRT_GUESS = float(0x5F3759DF)
NEWTON = 3
BIG = 3.0e38
TINY = 2.0 ** -100
W_TOP = 1024.0
EXPONENT = 0x7F800000
TWICE_BIAS = float(254 << 23)
IN_HI, IN_LO, HID_HI, HID_LO = range(4)

SEQ = EXPERTS * TOPK * PATCHES
HALF = SEQ // 2
UNROLL = P // PATCHES
BODIES = IMAGES // UNROLL

C_IDENT = 0
C_BAND = 128
C_OWN = 160
C_RANK = 166
C_COLS = 174


def vit_moe_lstm_kernel(nc, patches, tok_w, tok_b, qkv_w, proj_w, proj_b, router_w, router_b,
                        w_in, w_hid, gate_b, w_out, out_b, consts, out):
    with ExitStack() as ctx:
        def sb(name, shape, dt=F32):
            return ctx.enter_context(nc.sbuf_tensor(name, shape, dt))

        def sem(name):
            return ctx.enter_context(nc.semaphore(name))

        quads = [ctx.enter_context(nc.psum_tensor(f"quad{z}", [P, 4, 512], F32)) for z in range(2)]
        gate_bank = [[quads[0][:, 2 * g + par, :] for par in range(2)] for g in range(2)]
        turned = [quads[1][:, g, :] for g in range(2)]
        yT_bank, y_bank = (quads[1][:, 2 + n, 0:P] for n in range(2))

        cst = sb("cst", [P, C_COLS])
        ident = cst[:, C_IDENT:C_IDENT + P]
        tokw = sb("tokw", [P, KCH, P])
        tokb = sb("tokb", [P, 1])
        qkvw = sb("qkvw", [P, 3, P])
        projw = sb("projw", [P, P])
        projb = sb("projb", [P, P])
        rw_sb = sb("rw_sb", [P, EXPERTS])
        rb_sb = sb("rb_sb", [P, EXPERTS])
        w16 = sb("w16", [P, EXPERTS, 4, GATES], F16)
        stage = sb("stage", [P, 3, GATES])
        scl = sb("scl", [P, 10])
        unscale8 = sb("unscale8", [P, EXPERTS])
        unscale = sb("unscale", [P, 2])
        wo = sb("wo", [P, EXPERTS, P])
        bo2 = sb("bo2", [2 * EXPERTS, P])

        h2 = sb("h2", [P, TILES, P])
        xT = sb("xT", [P, 2, TOKENS], F16)
        maskT = sb("maskT", [2 * SEQ // PATCHES, TOKENS], F16)
        ckT = sb("ckT", [2 * SEQ // PATCHES, TOKENS])
        mix = sb("mix", [P, EXPERTS, TOKENS])

        sizes = {"pt": KCH * SUPER, "hT": SUPER, "h1": SUPER, "xn": SUPER, "xnT": SUPER, "qT": SUPER,
                 "kx": 2 * SUPER, "vt": SUPER, "s_a": SUPER, "s_b": SUPER, "s_e": SUPER, "s_p": SUPER,
                 "axT": 2 * SUPER, "oT": SUPER}
        work = sb("work", [P, sum(sizes.values())])
        B = []
        for flat in (work[:, :], mix[:, :, :].rearrange("p e n -> p (e n)")):
            at, one = 0, {}
            for name, size in sizes.items():
                one[name] = flat[:, at:at + size]
                at += size
            one["pt"] = one["pt"].rearrange("p (c n) -> p c n", c=KCH)
            for name in ("h1", "xn", "vt"):
                one[name + "_f"] = one[name]
                one[name] = one[name].rearrange("p (t c) -> p t c", c=P)
            one["ax"] = one["kx"]
            one["kx"] = one["kx"].rearrange("p (h n) -> p h n", h=2)
            B.append(one)
        st = sb("st", [P, STREAMS, 8, 32])
        sti = sb("sti", [P, STREAMS, ROW_TILES], I32)
        bn = sb("bn", [P, STREAMS, ROW_TILES, 6])
        lg = sb("lg", [P, 6, TILES, EXPERTS])
        rt = sb("rt", [P, 8, TILES])
        ck = sb("ck", [P, TILES, 4 * EXPERTS])

        xm = sb("xm", [P, 2, 2, SEQ], F16)
        h16 = sb("h16", [P, 2, 2, SEQ], F16)
        hs = sb("hs", [P, 2, SEQ])
        thc = sb("thc", [P, 2, P])
        hc = sb("hc", [P, SEQ])
        mst = sb("mst", [P, 2, 2 * SEQ], F16)
        gt = work[:, 0:12 * P].rearrange("p (g n) -> p g n", g=2)
        prod = work[:, 12 * P:16 * P].rearrange("p (g n) -> p g n", g=2)
        cst_s = work[:, 16 * P:16 * P + 4 * SEQ].rearrange("p (h n) -> p h n", h=2)
        yT = work[:, 24 * P:25 * P]

        scr_c = nc.dram_tensor("scr_c", [IMAGES, 16, PATCHES], F32).ap()
        scr_m = nc.dram_tensor("scr_m", [IMAGES, 16, PATCHES], F16).ap()

        names = """const_in tok_w_in w_small_in w_out_in stage_in stage_free diff_ready top_ready top_done
            prep_done ones_ready w_ready passed dve_done routed gap_ready gexp_ready ck_ready zeroed xT_ready
            xm_ready yT_psum yT_ready y_psum y_ready y_out""".split()
        S = {n: sem(n) for n in names}
        names = """patches_in patches_first embedded hT_ready h1_tr h1_ready xn_ready xn_tr xnT_ready qkv_ready
            q_copied v_copied kx_ready scores_ready split_ready shifted exp_ready p_ready ax_ready axT_ready
            heads_ready oT_ready proj_ready h2_ready xn2_ready xn2_tr xn2T_ready xT_hi xT_lo router_ready ck_tr
            ckT_ready scr_stored m_in c_in gates_ready ifg_ready o_ready prod_ready c_ready tr_ready thc_ready
            h_ready hid_ready low_ready hc_done mixed""".split()
        pair = {n: [sem(f"{n}{z}") for z in range(2)] for n in names}

        block = ctx.enter_context(nc.Block())

        patches_v = patches.rearrange("(c p) n -> p c n", p=P)
        out_v = out.rearrange("(t p) c -> p t c", p=P)

        @block.sync
        def _(sp):
            def load_patches(z, i):
                tokens = bass.ds((i * STREAMS + z) * SUPER, SUPER)
                for chunks, arrived in ((slice(0, KCH // 2), "patches_first"), (slice(KCH // 2, KCH), "patches_in")):
                    sp.dma_start(B[z]["pt"][:, chunks, :], patches_v[:, chunks, tokens]
                                 ).then_inc(pair[arrived][z], 16)

            sp.dma_start(tokw[:, :, :], tok_w.rearrange("(c p) n -> p c n", p=P)).then_inc(S["tok_w_in"], 16)
            load_patches(0, 0)
            sp.dma_start(tokb[:, :], tok_b).then_inc(S["w_small_in"], 16)
            sp.dma_start(cst[:, :], consts).then_inc(S["const_in"], 16)
            load_patches(1, 0)
            sp.dma_start(qkvw[:, :, :], qkv_w.rearrange("p (t n) -> p t n", t=3)).then_inc(S["w_small_in"], 16)
            sp.dma_start(projw[:, :], proj_w).then_inc(S["w_small_in"], 16)
            sp.dma_start(projb[:, :], proj_b.partition_broadcast(P)).then_inc(S["w_small_in"], 16)
            sp.dma_start(rw_sb[:, :], router_w).then_inc(S["w_small_in"], 16)
            sp.dma_start(rb_sb[:, :], router_b.partition_broadcast(P)).then_inc(S["w_small_in"], 16)

            def load_expert(e):
                for dst, src in ((stage[1:P, 0, :], w_in[bass.ds(e, 1), 1:P, :]),
                                 (stage[0:1, 0, :], gate_b[bass.ds(e, 1), :].unsqueeze(1)),
                                 (stage[:, 1, :], w_hid[bass.ds(e, 1), :, :])):
                    sp.dma_start(dst, src.rearrange("e p n -> (e p) n")).then_inc(S["stage_in"], 16)
                sp.dma_start(stage[1:P, 2, :], w_in[bass.ds(e, 1), 0, :].rearrange("e n -> (e n)")
                             .partition_broadcast(P - 1)).then_inc(S["stage_in"], 16)

            load_expert(0)
            sp.dma_start(wo[:, :, :], w_out.rearrange("e p n -> p e n")).then_inc(S["w_out_in"], 16)
            sp.dma_start(bo2[:, :], out_b).then_inc(S["w_out_in"], 16)
            for z in range(STREAMS):
                sp.wait_ge(pair["embedded"][z], 1)
                load_patches(z, 1)
            with sp.Fori(0, EXPERTS - 1) as e:
                sp.wait_ge(S["stage_free"], e + 1)
                sp.sem_inc(S["passed"])
                load_expert(e + 1)

            def load_masks(n, half):
                src = scr_m[bass.ds(2 * n, 2), :, :].rearrange("s k b -> (s k b)")
                sp.dma_start(mst[1:P, half, :], src.partition_broadcast(P - 1)).then_inc(pair["m_in"][half], 16)

            def load_weights(n, half):
                src = scr_c[bass.ds(2 * n, 2), :, :].rearrange("s k b -> (s k b)")
                sp.dma_start(cst_s[:, half, :], src.partition_broadcast(P)).then_inc(pair["c_in"][half], 16)

            def store_tile(t, n):
                sp.wait_ge(S["y_ready"], n)
                sp.sem_inc(S["passed"])
                sp.dma_start(out_v[:, bass.ds(t, 1), :], h2[:, bass.ds(t, 1), :]).then_inc(S["y_out"], 16)

            def store_routing(n):
                z, window = n % STREAMS, slice(n * SUPER, (n + 1) * SUPER)
                sp.wait_ge(pair["ckT_ready"][z], n // STREAMS + 1)
                for scr, src in ((scr_m, maskT[16:32, window]), (scr_c, ckT[0:16, window])):
                    sp.dma_start(scr[bass.ds(n * 32, 32), :, :].rearrange("s k b -> k s b"),
                                 src.rearrange("k (s b) -> k s b", b=PATCHES)).then_inc(pair["scr_stored"][z], 16)

            store_routing(0)
            store_routing(1)
            sp.wait_ge(pair["scr_stored"][0], 32)
            for half in range(2):
                load_masks(half, half)
            for half in range(2):
                load_weights(half, half)
            store_routing(2)
            store_routing(3)
            for z in range(STREAMS):
                sp.wait_ge(pair["scr_stored"][z], 32 * ROUNDS)

            def steps(j, first, last):
                for u in range(0, UNROLL, 4):
                    if last and u == UNROLL - 4:
                        break
                    s, n = j * UNROLL + u, j * (UNROLL // 2) + (u // 2 + 2)
                    sp.wait_ge(S["xm_ready"], s + 2)
                    load_masks(n, 0)
                    sp.wait_ge(S["xm_ready"], s + 4)
                    load_masks(n + 1, 1)
                    sp.wait_ge(pair["hc_done"][1], s + 2 + 2)
                    sp.sem_inc(S["passed"])
                    load_weights(n, 0)
                    sp.wait_ge(pair["hc_done"][1], s + 4 + 2)
                    sp.sem_inc(S["passed"])
                    load_weights(n + 1, 1)
                if not first:
                    store_tile(j - 1, j + 1)

            steps(0, True, False)
            with sp.Fori(1, BODIES - 1) as j:
                steps(j, False, False)
            steps(BODIES - 1, False, True)
            store_tile(BODIES - 1, BODIES + 1)
            sp.wait_ge(S["y_out"], 16 * BODIES)

        @block.tensor
        def _(pe):
            def tiles(z, bank):
                return [quads[z][:, bank, t * P:(t + 1) * P] for t in range(ROW_TILES)]

            def turn_rows(z, bank, rows, ready):
                for t in range(ROW_TILES):
                    m = pe.transpose(tiles(z, bank)[t], rows[t], ident)
                m.then_inc(pair[ready][z], 1)

            def embed(z, i):
                for c in range(KCH):
                    if c % (KCH // 2) == 0:
                        pe.wait_ge(pair["patches_in" if c else "patches_first"][z], (i + 1) * 16)
                    m = pe.matmul(quads[z][:, 0, :], tokw[:, c, :], B[z]["pt"][:, c, :],
                                  start=c == 0, stop=c == KCH - 1)
                m.then_inc(pair["embedded"][z], 1)

            def warm_up(z, bank, times):
                for _ in range(times):
                    pe.matmul(quads[z][:, bank, :], tokw[:, 0, :], tokw[:, 1:5, :], start=True, stop=True)

            pe.wait_ge(S["tok_w_in"], 16)
            for z in range(STREAMS):
                embed(z, 0)
            pe.wait_ge(S["w_small_in"], 16 * 6)
            pe.wait_ge(S["const_in"], 16)

            def attention(i, last):
                for z in range(STREAMS):
                    pe.wait_ge(pair["hT_ready"][z], i + 1)
                    turn_rows(z, 1, [B[z]["hT"][:, t * P:(t + 1) * P] for t in range(ROW_TILES)], "h1_tr")
                warm_up(0, 3, 4)
                for z in range(STREAMS):
                    pe.wait_ge(pair["xn_ready"][z], i + 1)
                    turn_rows(z, 2, [B[z]["xn"][:, t, :] for t in range(ROW_TILES)], "xn_tr")
                for z in range(STREAMS):
                    xnT = B[z]["xnT"]
                    pe.wait_ge(pair["xnT_ready"][z], i + 1)
                    pe.matmul(quads[z][:, 0, :], qkvw[:, 0, :], xnT, start=True, stop=True)
                    pe.matmul(quads[z][:, 1, :], qkvw[:, 1, :], xnT, start=True, stop=True)
                    for t in range(ROW_TILES):
                        m = pe.matmul(tiles(z, 3)[t], xnT[:, t * P:(t + 1) * P], qkvw[:, 2, :], start=True, stop=True)
                    m.then_inc(pair["qkv_ready"][z], 1)
                warm_up(1, 2, 1)
                for z in range(STREAMS):
                    qT, kx = B[z]["qT"], B[z]["kx"]
                    pe.wait_ge(pair["q_copied"][z], i + 1)
                    pe.wait_ge(pair["v_copied"][z], i + 1)
                    pe.wait_ge(pair["kx_ready"][z], i + 1)
                    pe.sem_inc(S["passed"])
                    for t in range(ROW_TILES):
                        for c in range(4):
                            for j in range(4):
                                tok = slice(t * P + 32 * j, t * P + 32 * j + 32)
                                m = pe.matmul(quads[z][32 * j:32 * j + 32, c, t * 64:(t + 1) * 64],
                                              qT[32 * c:32 * c + 32, tok], kx[32 * c:32 * c + 32, :, tok],
                                              start=True, stop=True)
                    m.then_inc(pair["scores_ready"][z], 1)
                if not last:
                    pe.wait_ge(pair["split_ready"][0], i + 1)
                    embed(0, i + 1)
                pe.wait_ge(pair["split_ready"][1], i + 1)
                pe.wait_ge(pair["exp_ready"][0], i * 2 + 2)
                if last:
                    warm_up(1, 3, KCH)
                else:
                    embed(1, i + 1)
                for z in range(STREAMS):
                    vt, axT = B[z]["vt"], B[z]["axT"].rearrange("p (r q) -> p r q", q=32)
                    if not last:
                        pe.wait_ge(pair["hT_ready"][z], i + 2)
                    pe.wait_ge(pair["axT_ready"][z], i + 1)
                    pe.sem_inc(S["passed"])
                    for t in range(ROW_TILES):
                        for j in range(4):
                            for c in range(4):
                                b0 = c * 8 + t * 2
                                m = pe.matmul(quads[z][32 * c:32 * c + 32, j, t * 64:(t + 1) * 64],
                                              vt[32 * j:32 * j + 32, t, 32 * c:32 * c + 32],
                                              axT[32 * j:32 * j + 32, b0:b0 + 2, :], start=True, stop=True)
                    m.then_inc(pair["heads_ready"][z], 1)
                for z in range(STREAMS):
                    pe.wait_ge(pair["oT_ready"][z], i + 1)
                    for t in range(ROW_TILES):
                        m = pe.matmul(tiles(z, 0)[t], B[z]["oT"][:, t * P:(t + 1) * P], projw[:, :],
                                      start=True, stop=True)
                    m.then_inc(pair["proj_ready"][z], 1)
                warm_up(0, 3, 4)
                for z in range(STREAMS):
                    pe.wait_ge(pair["xn2_ready"][z], i + 1)
                    turn_rows(z, 1, [B[z]["xn"][:, t, :] for t in range(ROW_TILES)], "xn2_tr")
                for z in range(STREAMS):
                    pe.wait_ge(pair["xn2T_ready"][z], i + 1)
                    for t in range(ROW_TILES):
                        m = pe.matmul(quads[z][:, 2, t * EXPERTS:(t + 1) * EXPERTS],
                                      B[z]["xnT"][:, t * P:(t + 1) * P], rw_sb[:, :], start=True, stop=True)
                    m.then_inc(pair["router_ready"][z], 1)

            with pe.Fori(0, ROUNDS - 1) as i:
                attention(i, False)
            attention(ROUNDS - 1, True)
            pe.wait_ge(S["ck_ready"], 1)
            for n in range(NSUPER):
                z, bank = n % STREAMS, 2 + n // STREAMS
                for t in range(ROW_TILES):
                    m = pe.transpose(tiles(z, bank)[t][0:4 * EXPERTS, :], ck[:, n * ROW_TILES + t, :], ident)
                m.then_inc(pair["ck_tr"][z], 1)

            warm_up(1, 0, 3)

            def gates(g, par):
                return gate_bank[g][par]

            def from_inputs(g, s, par, passes=range(3)):
                pe.wait_ge(S["xm_ready"], s + 1)
                for n in passes:
                    part, w = ((0, IN_HI), (0, IN_LO), (1, IN_HI))[n]
                    for q in range(4):
                        e = 4 * g + q
                        pe.matmul(gates(g, par)[32 * q:32 * q + 32], xm[:, par, part, 32 * e:32 * e + 32],
                                  w16[:, e, w, :], start=n == 0, stop=False)

            def from_hidden(g, s, par, passes=range(3)):
                for n in passes:
                    part, w = ((0, HID_HI), (0, HID_LO), (1, HID_HI))[n]
                    if n == 0:
                        pe.wait_ge(pair["h_ready"][g], s + 1)
                    if n == 2:
                        pe.wait_ge(pair["low_ready"][g], s + 1)
                    for q in range(4):
                        e = 4 * g + q
                        m = pe.matmul(gates(g, par)[32 * q:32 * q + 32], h16[:, 1 - par, part, 32 * e:32 * e + 32],
                                      w16[:, e, w, :], start=False, stop=n == 2)
                if n == 2:
                    m.then_inc(pair["gates_ready"][g], 1)

            def turn(g, s):
                pe.wait_ge(pair["o_ready"][g], s + 1)
                pe.transpose(turned[g][:, 0:P], gt[:, g, 3 * P:4 * P], ident)
                pe.wait_ge(pair["c_ready"][g], s + 1)
                pe.transpose(turned[g][:, P:2 * P], gt[:, g, 4 * P:5 * P], ident).then_inc(pair["tr_ready"][g], 1)

            pe.wait_ge(S["w_ready"], 1)
            pe.wait_ge(S["zeroed"], 1)
            for z in range(STREAMS):
                pe.wait_ge(pair["ckT_ready"][z], ROUNDS)
            from_inputs(0, 0, 0)
            from_inputs(1, 0, 0)
            from_hidden(0, 0, 0)

            def output(t, operands):
                tokens = bass.ds(t * P, P)
                for n in operands:
                    if n == 0:
                        pe.wait_ge(S["yT_ready"], t + 1)
                        for g in range(2):
                            pe.wait_ge(pair["mixed"][g], t * UNROLL + (UNROLL + 1))
                        pe.matmul(yT_bank, bo2[:, :], ckT[0:2 * EXPERTS, tokens], start=True, stop=False)
                    else:
                        m = pe.matmul(yT_bank, wo[:, n - 1, :], mix[:, n - 1, tokens], start=False, stop=n == EXPERTS)
                if EXPERTS in operands:
                    m.then_inc(S["yT_psum"], 1)

            def turn_output(t):
                pe.wait_ge(S["yT_ready"], t + 2)
                pe.wait_ge(S["y_ready"], t + 1)
                pe.transpose(y_bank, yT, ident).then_inc(S["y_psum"], 1)

            OUTPUT_AT = [(0, 1), (2,), (3,), (4,), (5,), (6,), (7, 8), ()]

            def steps(j, first, last):
                for u in range(UNROLL):
                    s, par = j * UNROLL + u, u % 2
                    end = last and u == UNROLL - 1
                    if not end:
                        from_inputs(0, s + 1, 1 - par, (0, 1))
                    from_hidden(1, s, par)
                    if not end:
                        from_inputs(0, s + 1, 1 - par, (2,))
                    turn(0, s)
                    if not first:
                        output(j - 1, OUTPUT_AT[u])
                        if u == UNROLL - 1:
                            turn_output(j - 1)
                    if not end:
                        from_inputs(1, s + 1, 1 - par)
                        from_hidden(0, s + 1, 1 - par, (0,))
                    turn(1, s)
                    if not end:
                        from_hidden(0, s + 1, 1 - par, (1, 2))

            steps(0, True, False)
            with pe.Fori(1, BODIES - 1) as j:
                steps(j, False, False)
            steps(BODIES - 1, False, True)
            output(BODIES - 1, range(EXPERTS + 1))
            turn_output(BODIES - 1)

        @block.scalar
        def _(act):
            def copy(z, i, after, dst, bank, ready):
                act.wait_ge(pair[after][z], i + 1)
                act.activation(dst, quads[z][:, bank, :], ACT.Copy).then_inc(pair[ready][z], 1)

            def own_head(z, dst, src, n, scale=C_OWN):
                return act.activation(dst, src, ACT.Identity, scale=cst[:, scale + n:scale + n + 1])

            act.wait_ge(S["w_small_in"], 16 * 6)
            act.wait_ge(S["const_in"], 16)

            def embedding(z, i):
                act.wait_ge(pair["embedded"][z], i + 1)
                act.activation(B[z]["hT"], quads[z][:, 0, :], ACT.Identity, bias=tokb[:, 0:1]
                               ).then_inc(pair["hT_ready"][z], 1)

            for z in range(STREAMS):
                embedding(z, 0)

            def attention(i, last):
                for z in range(STREAMS):
                    copy(z, i, "h1_tr", B[z]["h1_f"], 1, "h1_ready")
                for z in range(STREAMS):
                    copy(z, i, "xn_tr", B[z]["xnT"], 2, "xnT_ready")
                for z in range(STREAMS):
                    act.wait_ge(pair["qkv_ready"][z], i + 1)
                    own_head(z, B[z]["kx"][:, 0, :], quads[z][:, 1, :], 0)
                    own_head(z, B[z]["kx"][:, 1, :], quads[z][:, 1, :], 1).then_inc(pair["kx_ready"][z], 1)
                for z in range(STREAMS):
                    act.wait_ge(pair["scores_ready"][z], i + 1)
                    s_all = quads[z][:, :, 0:256].rearrange("p c (r i k) -> p c r i k", i=2, k=PATCHES)
                    for n, dst in enumerate(("s_b", "s_e")):
                        ins = own_head(z, B[z][dst].rearrange("p (c r k) -> p c r k", c=4, k=PATCHES),
                                       s_all[:, :, :, n, :], n + 2)
                    ins.then_inc(pair["split_ready"][z], 1)
                for w in range(2):
                    for z in range(STREAMS):
                        act.wait_ge(pair["shifted"][z], i * 2 + (w + 1))
                        act.activation(B[z]["s_e"], B[z]["s_b"], ACT.Exp).then_inc(pair["exp_ready"][z], 1)
                    if w == 0 and not last:
                        embedding(0, i + 1)
                for z in range(STREAMS):
                    act.wait_ge(pair["p_ready"][z], i + 1)
                    for n in range(2):
                        ins = own_head(z, B[z]["ax"].rearrange("p (r k) -> p r k", k=32)
                                       [:, :, n * PATCHES:(n + 1) * PATCHES],
                                       B[z]["s_p"].rearrange("p (r k) -> p r k", k=PATCHES), n + 2)
                    ins.then_inc(pair["ax_ready"][z], 1)
                if not last:
                    embedding(1, i + 1)
                for z in range(STREAMS):
                    act.wait_ge(pair["h2_ready"][z], i + 1)
                    act.activation(h2[:, bass.ds((i * STREAMS + z) * ROW_TILES, ROW_TILES), :], B[z]["h1"], ACT.Copy)
                for z in range(STREAMS):
                    copy(z, i, "xn2_tr", B[z]["xnT"], 1, "xn2T_ready")
                    act.wait_ge(pair["xn2T_ready"][z], i + 1)
                    act.activation(xT[:, 0, bass.ds((i * STREAMS + z) * SUPER, SUPER)], B[z]["xnT"], ACT.Copy
                                   ).then_inc(pair["xT_hi"][z], 1)

            with act.Fori(0, ROUNDS - 1) as i:
                attention(i, False)
            attention(ROUNDS - 1, True)
            act.wait_ge(S["gap_ready"], 1)
            act.activation(rt[:, 7, :], rt[:, 6, :], ACT.Exp).then_inc(S["gexp_ready"], 1)
            for n in range(NSUPER):
                z, bank, window = n % STREAMS, 2 + n // STREAMS, slice(n * SUPER, (n + 1) * SUPER)
                act.wait_ge(pair["ck_tr"][z], n // STREAMS + 1)
                act.activation(maskT[0:32, window], quads[z][0:32, bank, :], ACT.Copy)
                act.activation(ckT[:, window], quads[z][0:32, bank, :], ACT.Copy).then_inc(pair["ckT_ready"][z], 1)

            def gate_tanh(g, s, par, gates, ready):
                if ready == "ifg_ready":
                    act.wait_ge(pair["gates_ready"][g], s + 1)
                act.activation(gt[:, g, gates], gate_bank[g][par][:, gates], ACT.Tanh, scale=unscale[:, g:g + 1]
                               ).then_inc(pair[ready][g], 1)

            def cell_tanh(g, s):
                act.wait_ge(pair["tr_ready"][g], s + 1)
                act.activation(thc[:, g, :], turned[g][:, P:2 * P], ACT.Tanh, scale=0.5
                               ).then_inc(pair["thc_ready"][g], 1)

            IFG, O = slice(0, 3 * P), slice(3 * P, 4 * P)
            act.wait_ge(S["w_ready"], 1)
            gate_tanh(0, 0, 0, IFG, "ifg_ready")

            def copy_output(t):
                act.wait_ge(S["yT_psum"], t + 1)
                act.activation(yT, yT_bank, ACT.Copy).then_inc(S["yT_ready"], 1)

            def steps(j, first, last):
                for u in range(UNROLL):
                    s, par = j * UNROLL + u, u % 2
                    gate_tanh(0, s, par, O, "o_ready")
                    if u == UNROLL - 1 and not first:
                        copy_output(j - 1)
                    gate_tanh(1, s, par, IFG, "ifg_ready")
                    cell_tanh(0, s)
                    gate_tanh(1, s, par, O, "o_ready")
                    cell_tanh(1, s)
                    if not (last and u == UNROLL - 1):
                        gate_tanh(0, s + 1, 1 - par, IFG, "ifg_ready")

            steps(0, True, False)
            with act.Fori(1, BODIES - 1) as j:
                steps(j, False, False)
            steps(BODIES - 1, False, True)
            copy_output(BODIES - 1)

        @block.vector
        def _(dve):
            LINKS = 86
            dve.wait_ge(S["const_in"], 16)
            dve.wait_ge(S["w_small_in"], 16 * 6)

            def weights_top(e):
                dve.wait_ge(S["diff_ready"], e + 1)
                power, minus_inverse, top = (scl[:, n:n + 1] for n in (0, 1, 8))
                chain = (lambda: dve.tensor_reduce(top, stage[:, 0:2, :].rearrange("p a n -> p (a n)"), AX_X, ALU.max,
                                                   apply_absolute_value=True),
                         lambda: dve.tensor_scalar(top, top, TINY, None, ALU.max),
                         lambda: dve.tensor_scalar(power.bitcast(I32), top.bitcast(I32), EXPONENT, None,
                                                   ALU.bitwise_and),
                         lambda: dve.tensor_scalar(top.bitcast(I32), power.bitcast(I32), -1.0, TWICE_BIAS,
                                                   ALU.mult, ALU.add),
                         lambda: dve.tensor_scalar(minus_inverse, top, -1.0, None, ALU.mult))
                for m, op in enumerate(chain):
                    if m < len(chain) - 1:
                        op().then_inc(S["top_done"], 1)
                        dve.wait_ge(S["top_done"], e * (len(chain) - 1) + (m + 1))
                    else:
                        op().then_inc(S["top_ready"], 1)

            TOPS = 4

            def attention(i, last):
                count, before = [0], [None, None]

                def one(z, op, after=None, times=(1, 1), ready=None):
                    if before[z] is not None:
                        done, per_round, n = before[z]
                        dve.wait_ge(done, i * per_round + n)
                    if after is not None:
                        dve.wait_ge(pair[after][z], i * times[0] + times[1])
                    ins = op(z)
                    if ready is not None:
                        before[z] = (pair[ready][z], times[0], times[1])
                        ins.then_inc(pair[ready][z], 1)
                    else:
                        count[0] += 1
                        before[z] = (S["dve_done"], LINKS, count[0])
                        ins.then_inc(S["dve_done"], 1)

                def both(op, after=None, times=(1, 1), ready=None):
                    for z in range(STREAMS):
                        one(z, op, after, times, ready)

                def joint(op, waits=True):
                    if waits:
                        done, per_round, n = before[1]
                        dve.wait_ge(done, i * per_round + n)
                    count[0] += 1
                    before[0] = before[1] = (S["dve_done"], LINKS, count[0])
                    op().then_inc(S["dve_done"], 1)

                def tt(out, a, b, op):
                    return dve.tensor_tensor(out, a, b, op)

                def ts(out, a, s1, s2, op0, op1=None):
                    if op1 is None:
                        return dve.tensor_scalar(out, a, s1, None, op0)
                    return dve.tensor_scalar(out, a, s1, s2, op0, op1)

                def stt(out, a, s1, b, op0, op1):
                    return dve.scalar_tensor_tensor(out=out, in0=a, scalar=s1, in1=b, op0=op0, op1=op1)

                def small(z, n, width=ROW_TILES):
                    return st[:, z, n, 0:width]

                def layernorm(src, after, ready, src_op=None):
                    for z in range(STREAMS):
                        if src_op is not None:
                            one(z, src_op, after, ready="h2_ready")
                            dve.wait_ge(pair["h2_ready"][z], i + 1)
                        elif after is not None:
                            dve.wait_ge(pair[after][z], i + 1)
                        for t in range(ROW_TILES):
                            count[0] += 1
                            dve.bn_stats(bn[:, z, t, :], B[z][src][:, t, :]).then_inc(S["dve_done"], 1)
                        before[z] = (S["dve_done"], LINKS, count[0])
                    even, odd, m2 = bn[:, :, :, 1], bn[:, :, :, 4], (bn[:, :, :, 2], bn[:, :, :, 5])
                    total, delta, var, y, t = (st[:, :, n, 0:ROW_TILES] for n in (0, 1, 3, 4, 5))
                    joint(lambda: tt(delta, even, odd, ALU.subtract))
                    joint(lambda: tt(var, *m2, ALU.add), False)
                    joint(lambda: tt(total, even, odd, ALU.add), False)
                    joint(lambda: stt(delta, delta, 0.25 * P, delta, ALU.mult, ALU.mult))
                    joint(lambda: ts(total, total, 0.5, None, ALU.mult), False)
                    joint(lambda: tt(var, delta, var, ALU.add))
                    joint(lambda: ts(var, var, 1.0 / P, LN_EPS, ALU.mult, ALU.add))
                    joint(lambda: ts(sti[:, :, :], var.bitcast(I32), 1, None, ALU.logical_shift_right))
                    joint(lambda: ts(y.bitcast(I32), sti[:, :, :], -1.0, RSQRT_GUESS, ALU.mult, ALU.add))
                    for _ in range(NEWTON):
                        joint(lambda: stt(t, y, -0.5, y, ALU.mult, ALU.mult))
                        joint(lambda: tt(t, t, var, ALU.mult))
                        joint(lambda: stt(y, t, 1.5, y, ALU.add, ALU.mult))
                    dve.wait_ge(S["dve_done"], i * LINKS + count[0])
                    for z in range(STREAMS):
                        for t in range(ROW_TILES):
                            ins = ts(B[z]["xn"][:, t, :], B[z][src][:, t, :], st[:, z, 0, t:t + 1],
                                     st[:, z, 4, t:t + 1], ALU.subtract, ALU.mult)
                        ins.then_inc(pair[ready][z], 1)
                        before[z] = (pair[ready][z], 1, 1)

                def keys(a):
                    return a.rearrange("p (r k) -> p r k", k=PATCHES)

                def per_row(z, n):
                    return small(z, n, 32).unsqueeze(2).to_broadcast([P, 32, PATCHES])

                def own_col(n):
                    return cst[:, C_OWN + n:C_OWN + n + 1]

                layernorm("h1", "h1_ready", "xn_ready")
                both(lambda z: tt(B[z]["h1"], B[z]["h1"], projb[:, :].unsqueeze(1).to_broadcast([P, ROW_TILES, P]),
                                  ALU.add))
                for z in range(STREAMS):
                    one(z, lambda z: dve.tensor_copy(B[z]["qT"], quads[z][:, 0, :]), "qkv_ready", ready="q_copied")
                    one(z, lambda z: dve.tensor_copy(B[z]["vt_f"], quads[z][:, 3, :]), ready="v_copied")
                weights_top(i * TOPS + 1)
                def shift(z, w):
                    band = cst[:, C_BAND + w * PATCHES:C_BAND + (w + 1) * PATCHES] \
                        .unsqueeze(1).to_broadcast([P, 32, PATCHES])
                    one(z, lambda z: tt(keys(B[z]["s_b"]), keys(B[z]["s_a"]), band, ALU.add))
                    one(z, lambda z: dve.tensor_reduce(small(z, 0, 32), keys(B[z]["s_b"]), AX_X, ALU.max))
                    one(z, lambda z: tt(keys(B[z]["s_b"]), keys(B[z]["s_b"]), per_row(z, 0), ALU.subtract),
                        None, (2, w + 1), "shifted")

                for z in range(STREAMS):
                    one(z, lambda z: tt(B[z]["s_a"], B[z]["s_b"], B[z]["s_e"], ALU.add), "split_ready")
                    shift(z, 0)
                for w in range(2):
                    both(lambda z: dve.tensor_reduce(small(z, 1, 32), keys(B[z]["s_e"]), AX_X, ALU.add),
                         "exp_ready", (2, w + 1))
                    both(lambda z: dve.reciprocal(small(z, 2, 32), small(z, 1, 32)))
                    dst = "s_p" if w == 0 else "s_e"
                    both(lambda z: tt(keys(B[z][dst]), keys(B[z]["s_e"]), per_row(z, 2), ALU.mult))
                    if w == 0 and not last:
                        weights_top(i * TOPS + 2)
                    if w == 0:
                        for z in range(STREAMS):
                            shift(z, 1)
                both(lambda z: tt(B[z]["s_p"], B[z]["s_p"], B[z]["s_e"], ALU.add), ready="p_ready")
                both(lambda z: dve.transpose(B[z]["axT"], B[z]["ax"]), "ax_ready", ready="axT_ready")
                weights_top(i * TOPS + (2 if last else 3))
                def parts(z, j):
                    return (quads[z][:, j, 0:256].rearrange("p (t h q) -> p t h q", t=4, h=2),
                            B[z]["oT"].rearrange("p (t j q) -> p t j q", t=4, j=4)[:, :, j, :])

                for z in range(STREAMS):
                    dve.wait_ge(pair["heads_ready"][z], i + 1)
                    for j in range(4):
                        heads, own = parts(z, j)
                        count[0] += 1
                        ts(own, heads[:, :, 0, :], own_col(4), None, ALU.mult).then_inc(S["dve_done"], 1)
                    for j in range(4):
                        heads, own = parts(z, j)
                        dve.wait_ge(S["dve_done"], i * LINKS + (count[0] - 3 + j))
                        ins = stt(own, heads[:, :, 1, :], own_col(5), own, ALU.mult, ALU.add)
                    ins.then_inc(pair["oT_ready"][z], 1)
                    before[z] = (pair["oT_ready"][z], 1, 1)
                layernorm("h1", "proj_ready", "xn2_ready",
                          lambda z: tt(B[z]["h1_f"], B[z]["h1_f"], quads[z][:, 0, :], ALU.add))
                weights_top(i * TOPS + (3 if last else 4))
                for_all = lambda z: bass.ds((i * STREAMS + z) * SUPER, SUPER)
                both(lambda z: tt(xT[:, 1, for_all(z)], B[z]["xnT"], xT[:, 0, for_all(z)], ALU.subtract), "xT_hi",
                     ready="xT_lo")
                both(lambda z: tt(lg[:, LOGITS, bass.ds((i * STREAMS + z) * ROW_TILES, ROW_TILES)],
                                  quads[z][:, 2, 0:32].rearrange("p (t e) -> p t e", e=EXPERTS),
                                  rb_sb[:, :].unsqueeze(1).to_broadcast([P, ROW_TILES, EXPERTS]), ALU.add),
                     "router_ready")
                assert last or count[0] == LINKS, count[0]

            LOGITS, SCORE, FIRST, SECOND, REST, EQUAL = range(6)
            weights_top(0)
            with dve.Fori(0, ROUNDS - 1) as i:
                attention(i, False)
            attention(ROUNDS - 1, True)

            chained = [0]

            def chain(ins):
                chained[0] += 1
                ins.then_inc(S["routed"], 1)
                dve.wait_ge(S["routed"], chained[0])

            def cols(n):
                return rt[:, n, :].unsqueeze(2).to_broadcast([P, TILES, EXPERTS])

            rank = cst[:, C_RANK:C_RANK + EXPERTS].unsqueeze(1).to_broadcast([P, TILES, EXPERTS])
            dve.wait_ge(S["dve_done"], ROUNDS * LINKS)
            for n, (src, hot) in enumerate(((LOGITS, FIRST), (REST, SECOND))):
                chain(dve.tensor_reduce(rt[:, n, :], lg[:, src], AX_X, ALU.max))
                chain(dve.tensor_tensor(lg[:, EQUAL], lg[:, src], cols(n), ALU.is_equal))
                chain(dve.tensor_tensor(lg[:, SCORE], lg[:, EQUAL], rank, ALU.mult))
                chain(dve.tensor_reduce(rt[:, 2, :], lg[:, SCORE], AX_X, ALU.max))
                chain(dve.tensor_tensor(lg[:, hot], lg[:, SCORE], cols(2), ALU.is_equal))
                if n == 0:
                    chain(dve.scalar_tensor_tensor(out=lg[:, REST], in0=lg[:, FIRST], scalar=-BIG,
                                                   in1=lg[:, LOGITS], op0=ALU.mult, op1=ALU.add))
            dve.tensor_tensor(rt[:, 6, :], rt[:, 1, :], rt[:, 0, :], ALU.subtract).then_inc(S["gap_ready"], 1)

            def choice(k, rows):
                return ck[:, :, rows:rows + 16].rearrange("p t (e k) -> p t e k", k=2)[:, :, :, k]

            for k, hot in enumerate((FIRST, SECOND)):
                chain(dve.tensor_copy(choice(k, 16), lg[:, hot]))
            dve.wait_ge(S["gexp_ready"], 1)
            chain(dve.tensor_scalar(rt[:, 3, :], rt[:, 7, :], 1.0, None, ALU.add))
            chain(dve.reciprocal(rt[:, 4, :], rt[:, 3, :]))
            chain(dve.tensor_tensor(rt[:, 5, :], rt[:, 7, :], rt[:, 4, :], ALU.mult))
            for k, hot in enumerate((FIRST, SECOND)):
                chain(dve.scalar_tensor_tensor(out=choice(k, 0), in0=lg[:, hot], scalar=0.5, in1=cols(4 + k),
                                               op0=ALU.mult, op1=ALU.mult))
            dve.sem_inc(S["ck_ready"])

            for z in range(STREAMS):
                dve.wait_ge(pair["xT_lo"][z], ROUNDS)
            dve.memset(xT[0:1, 0, :], 1.0).then_inc(S["xT_ready"], 1)
            dve.memset(xT[0:1, 1, :], 0.0).then_inc(S["xT_ready"], 1)
            dve.memset(gt[:, :, 4 * P:], 0.0).then_inc(S["zeroed"], 1)
            dve.memset(h16[:, :, 0, 0:HALF], 0.0).then_inc(pair["h_ready"][0], 1)
            dve.memset(h16[:, :, 0, HALF:], 0.0).then_inc(pair["h_ready"][1], 1)
            for g in range(2):
                dve.memset(h16[:, :, 1, g * HALF:(g + 1) * HALF], 0.0).then_inc(pair["low_ready"][g], 1)
            dve.memset(prod[:, 0, 0:P], 0.0).then_inc(S["y_ready"], 1)
            dve.memset(yT, 0.0).then_inc(S["yT_ready"], 1)
            dve.wait_ge(S["zeroed"], 1)
            dve.wait_ge(S["y_ready"], 1)
            dve.wait_ge(S["yT_ready"], 1)
            for g in range(2):
                dve.wait_ge(pair["h_ready"][g], 1)
                dve.wait_ge(pair["low_ready"][g], 1)

            def products(g, s):
                dve.wait_ge(pair["ifg_ready"][g], s + 1)
                dve.scalar_tensor_tensor(out=prod[:, g, :].rearrange("p (a u) -> p a u", u=P),
                                         in0=gt[:, g, 0:2 * P].rearrange("p (a u) -> p a u", u=P), scalar=1.0,
                                         in1=gt[:, g, 2 * P:].rearrange("p (a u) -> p a u", a=2)[:, :, 0:P],
                                         op0=ALU.add, op1=ALU.mult).then_inc(pair["prod_ready"][g], 1)

            def cell(g, s):
                dve.wait_ge(pair["prod_ready"][g], s + 1)
                dve.scalar_tensor_tensor(out=gt[:, g, 4 * P:5 * P], in0=prod[:, g, P:], scalar=0.5,
                                         in1=prod[:, g, 0:P], op0=ALU.mult, op1=ALU.add
                                         ).then_inc(pair["c_ready"][g], 1)

            def cols(g):
                return slice(g * HALF, (g + 1) * HALF)

            def hidden_high(g, s, par):
                dve.wait_ge(pair["thc_ready"][g], s + 1)
                dve.scalar_tensor_tensor(out=h16[:, par, 0, cols(g)], in0=turned[g][:, 0:P], scalar=1.0,
                                         in1=thc[:, g, :], op0=ALU.add, op1=ALU.mult
                                         ).then_inc(pair["h_ready"][g], 1)

            def hidden_low(g, s, par):
                dve.wait_ge(pair["hc_done"][g], s + 1)
                dve.scalar_tensor_tensor(out=hs[:, par, cols(g)], in0=turned[g][:, 0:P], scalar=1.0,
                                         in1=thc[:, g, :], op0=ALU.add, op1=ALU.mult
                                         ).then_inc(pair["hid_ready"][g], 1)
                dve.wait_ge(pair["h_ready"][g], s + 2)
                dve.wait_ge(pair["hid_ready"][g], s + 1)
                dve.tensor_tensor(h16[:, par, 1, cols(g)], hs[:, par, cols(g)], h16[:, par, 0, cols(g)],
                                  ALU.subtract).then_inc(pair["low_ready"][g], 1)

            def masked_input(s, par, half, in_half, count):
                dve.wait_ge(pair["m_in"][half], count)
                x_s = xT[:, :, bass.ds(s * PATCHES, PATCHES)].unsqueeze(2).to_broadcast([P, 2, 16, PATCHES])
                m_s = mst[:, half, in_half * SEQ:(in_half + 1) * SEQ].unsqueeze(1).to_broadcast([P, 2, SEQ])
                dve.tensor_tensor(xm[:, par, :, :].rearrange("p a (k b) -> p a k b", b=PATCHES), x_s,
                                   m_s.rearrange("p a (k b) -> p a k b", b=PATCHES), ALU.mult
                                   ).then_inc(S["xm_ready"], 1)

            dve.wait_ge(S["xT_ready"], 2)
            dve.wait_ge(S["ones_ready"], 5)
            masked_input(0, 0, 0, 0, 16)
            masked_input(1, 1, 0, 1, 16)
            products(0, 0)
            cell(0, 0)

            def add_output(t):
                dve.wait_ge(S["y_psum"], t + 1)
                row = h2[:, bass.ds(t, 1), :]
                dve.tensor_tensor(row, y_bank.unsqueeze(1), row, ALU.add).then_inc(S["y_ready"], 1)

            def steps(j, first, last):
                for u in range(UNROLL):
                    s, par = j * UNROLL + u, u % 2
                    if u < UNROLL - 2 or not last:
                        n = u // 2 + 1
                        masked_input(s + 2, par, n % 2, par, j * (16 * UNROLL // 4) + (n // 2 + 1) * 16)
                    products(1, s)
                    hidden_high(0, s, par)
                    cell(1, s)
                    hidden_low(0, s, par)
                    hidden_high(1, s, par)
                    hidden_low(1, s, par)
                    if not (last and u == UNROLL - 1):
                        products(0, s + 1)
                        cell(0, s + 1)
                if not first:
                    add_output(j - 1)

            steps(0, True, False)
            with dve.Fori(1, BODIES - 1) as j:
                steps(j, False, False)
            steps(BODIES - 1, False, True)
            add_output(BODIES - 1)

        @block.gpsimd
        def _(pool):
            for g in range(2):
                pool.memset(hs[:, g, :], 0.0).then_inc(pair["hc_done"][g], 2)
                pool.memset(hc[:, g * HALF:(g + 1) * HALF], 0.0).then_inc(pair["mixed"][g], 1)
            pool.memset(mst[0:1, :, :], 1.0).then_inc(S["ones_ready"], 1)
            pool.memset(scl[:, 7:8], 1.0 / W_TOP).then_inc(S["ones_ready"], 1)
            pool.memset(scl[:, 6:7], -W_TOP).then_inc(S["ones_ready"], 1)
            pool.memset(stage[0:1, 2, :], 0.0).then_inc(S["ones_ready"], 1)
            pool.memset(scl[:, 9:10], 0.0).then_inc(S["ones_ready"], 1)
            pool.wait_ge(S["ones_ready"], 5)
            STEPS = 9
            with pool.Fori(0, EXPERTS) as e:
                count = [0]

                def step(ins):
                    count[0] += 1
                    ins.then_inc(S["prep_done"], 1)
                    pool.wait_ge(S["prep_done"], e * STEPS + count[0])
                    pool.sem_inc(S["passed"])

                pool.wait_ge(S["stage_in"], (e + 1) * 64)
                pool.sem_inc(S["passed"])
                both, top = stage[:, 0:2, :], [scl[:, n:n + 1] for n in range(8)]
                zero2 = scl[:, 9:10].unsqueeze(2).to_broadcast([P, 2, GATES])
                step(pool.tensor_tensor(stage[:, 0, :], stage[:, 0, :], stage[:, 2, :], ALU.subtract))
                pool.sem_inc(S["diff_ready"])
                pool.wait_ge(S["top_ready"], e + 1)
                pool.sem_inc(S["passed"])
                step(pool.partition_all_reduce(scl[:, 2:4], scl[:, 0:2], P, bass.bass_isa.ReduceOp.max))
                step(pool.tensor_tensor(unscale8[:, bass.ds(e, 1)], top[2], top[7], ALU.mult))
                step(pool.tensor_tensor(top[5], top[6], top[3], ALU.mult))
                step(pool.tensor_scalar(stage[:, 0, :], stage[:, 0, :], top[5], 0.5, ALU.mult, ALU.mult))
                step(pool.tensor_scalar(stage[:, 1, :], stage[:, 1, :], top[5], 0.25, ALU.mult, ALU.mult))
                cell_gate = stage[:, 0:2, 2 * P:3 * P]
                step(pool.tensor_scalar(cell_gate, cell_gate, 2.0, None, ALU.mult))
                high, low = (w16[:, bass.ds(e, 1), n::2, :].rearrange("p e a n -> p (e a) n") for n in range(2))
                step(pool.tensor_tensor(high, both, zero2, ALU.add))
                step(pool.tensor_tensor(low, both, high, ALU.subtract))
                pool.sem_inc(S["stage_free"])
                assert count[0] == STEPS
            for e in range(EXPERTS):
                q = slice(32 * (e % 4), 32 * (e % 4) + 32)
                pool.tensor_copy(unscale[q, e // 4:e // 4 + 1], unscale8[q, e:e + 1]).then_inc(S["ones_ready"], 1)
            pool.wait_ge(S["w_out_in"], 32)
            pool.tensor_scalar(bo2[:, :], bo2[:, :], 2.0, None, ALU.mult).then_inc(S["ones_ready"], 1)
            pool.wait_ge(S["ones_ready"], 5 + EXPERTS + 1)
            pool.memset(scl[:, 0:1], 0.0).then_inc(S["w_ready"], 1)

            def weighted_state(g, s, par, half, in_half, count):
                cols = slice(g * HALF, (g + 1) * HALF)
                if g == 0:
                    pool.wait_ge(pair["c_in"][half], count)
                pool.wait_ge(pair["hid_ready"][g], s + 1)
                pool.wait_ge(pair["mixed"][g], s + 1)
                pool.tensor_tensor(hc[:, cols], hs[:, par, cols],
                                   cst_s[:, half, in_half * SEQ + g * HALF:in_half * SEQ + (g + 1) * HALF],
                                   ALU.mult).then_inc(pair["hc_done"][g], 1)
                pool.wait_ge(pair["hc_done"][g], s + 1 + 2)
                by_choice = hc[:, cols].rearrange("p (e k b) -> p e k b", k=2, b=PATCHES)
                pool.tensor_tensor(mix[:, 4 * g:4 * g + 4, bass.ds(s * PATCHES, PATCHES)], by_choice[:, :, 0, :],
                                   by_choice[:, :, 1, :], ALU.add).then_inc(pair["mixed"][g], 1)

            def steps(j, last):
                for u in range(UNROLL):
                    s, par = j * UNROLL + u, u % 2
                    for g in range(2):
                        weighted_state(g, s, par, u // 2 % 2, par, j * (16 * UNROLL // 4) + (u // 4 + 1) * 16)

            with pool.Fori(0, BODIES - 1) as j:
                steps(j, False)
            steps(BODIES - 1, True)


def kernel(x, L0_tok_w, L0_tok_b, L0_attn_qkv_w, L0_attn_proj_w, L0_attn_proj_b, L0_ffn_router_w,
           L0_ffn_router_b, L0_ffn_Wi, L0_ffn_Wh, L0_ffn_b, L0_ffn_Wo, L0_ffn_bo):
    import numpy as _np
    import concourse.bacc as _bacc
    from concourse import mybir as _mybir
    from concourse.bass_utils import run_bass_kernel_spmd as _run

    consts = _np.zeros((P, C_COLS), _np.float32)
    consts[:, C_IDENT:C_IDENT + P] = _np.eye(P, dtype=_np.float32)
    q = _np.arange(P)[:, None] % PATCHES
    k = _np.arange(PATCHES)[None, :]
    for w, size in enumerate((9, 17)):
        consts[:, C_BAND + w * PATCHES:C_BAND + (w + 1) * PATCHES] = _np.where(abs(q - k) <= size // 2, 0.0, -BIG)
    odd = (_np.arange(P) // PATCHES) % 2
    for n, scale in enumerate((DH ** -0.5, 1.0, 0.5)):
        consts[:, C_OWN + 2 * n] = (1 - odd) * scale
        consts[:, C_OWN + 2 * n + 1] = odd * scale
    consts[:, C_RANK:C_RANK + EXPERTS] = EXPERTS - _np.arange(EXPERTS)

    a = _np.asarray
    side = 4
    patches = a(x).reshape(IMAGES, 3, side, 16, side, 16).transpose(1, 3, 5, 0, 2, 4).reshape(KCH * P, TOKENS)
    laid = [
        ("patches", patches),
        ("tok_w", a(L0_tok_w).T),
        ("tok_b", a(L0_tok_b).reshape(P, 1)),
        ("qkv_w", a(L0_attn_qkv_w).T),
        ("proj_w", a(L0_attn_proj_w).T),
        ("proj_b", a(L0_attn_proj_b)),
        ("router_w", a(L0_ffn_router_w)),
        ("router_b", a(L0_ffn_router_b)),
        ("w_in", a(L0_ffn_Wi)),
        ("w_hid", a(L0_ffn_Wh)),
        ("gate_b", a(L0_ffn_b)),
        ("w_out", a(L0_ffn_Wo)),
        ("out_b", a(L0_ffn_bo).repeat(TOPK, axis=0)),
        ("consts", consts),
    ]
    nc = _bacc.Bacc("TRN2", target_bir_lowering=False, num_devices=1)
    arrays, args = {}, []
    for name, arr in laid:
        arr = _np.ascontiguousarray(arr)
        arrays[f"in_{name}_dram"] = arr
        args.append(nc.dram_tensor(f"in_{name}_dram", arr.shape, _mybir.dt.from_np(arr.dtype),
                                   kind="ExternalInput").ap())
    args.append(nc.dram_tensor("out_dram", (TOKENS, P), _mybir.dt.float32, kind="ExternalOutput").ap())
    vit_moe_lstm_kernel(nc, *args)
    r = _run(nc, [arrays], core_ids=[0])
    return r.results[0]["out_dram"].reshape(IMAGES, PATCHES, P)
```
